# Optimizing a Trainium2 kernel written in Bass

```python
import numpy as np
import jax
import jax.numpy as jnp

def _softmax(x, axis=-1):
    return jax.nn.softmax(x, axis=axis)

def _gelu(x):
    return jax.nn.gelu(x, approximate=True)

def _silu(x):
    return jax.nn.silu(x)

def _sigmoid(x):
    return jax.nn.sigmoid(x)

def _layernorm(x, axis=-1, eps=1e-05):
    m = jnp.mean(x, axis=axis, keepdims=True)
    v = jnp.var(x, axis=axis, keepdims=True)
    return (x - m) / jnp.sqrt(v + eps)

def _scatter_add(tgt, idx, src, axis=0):
    return tgt.at[idx].add(src)

def _segment_sum(src, seg, n):
    return jax.ops.segment_sum(src, seg, n)
kernel_name = 'mk_adaln_d1_jaxref_r4_be863a'

def setup_inputs(seed: int=0):
    np.random.seed(seed)
    _w = jnp.asarray

    def _L0_attn_setup():
        import jax, jax.numpy as jnp
        import numpy as np
        HIDDEN = 256
        D_INNER = 512
        DT_RANK = 64
        STATE = 16
        KCONV = 4

        def _selective_scan(u, delta, A, B, C):
            deltaA = jnp.exp(delta[..., None] * A)
            dBu = (delta * u)[..., None] * B[:, :, None, :]
            deltaA_t = jnp.moveaxis(deltaA, 1, 0)
            dBu_t = jnp.moveaxis(dBu, 1, 0)
            C_t = jnp.moveaxis(C, 1, 0)

            def step(h, inp):
                dA_i, dBu_i, C_i = inp
                h = dA_i * h + dBu_i
                y = jnp.einsum('bdn,bn->bd', h, C_i)
                return (h, y)
            h0 = jnp.zeros(u.shape[:1] + u.shape[2:] + (A.shape[1],), dtype=u.dtype)
            _, ys = jax.lax.scan(step, h0, (deltaA_t, dBu_t, C_t))
            return jnp.moveaxis(ys, 0, 1)
        key = jax.random.key(seed)
        ks = jax.random.split(key, 9)
        s = lambda k, shape, sc=0.02: jax.random.normal(k, shape, dtype=jnp.float32) * sc
        return {'x': jax.random.normal(ks[0], (2, 256, HIDDEN), dtype=jnp.float32), 'in_proj_w': s(ks[1], (2 * D_INNER, HIDDEN)), 'conv_w': s(ks[2], (D_INNER, 1, KCONV), 0.2), 'conv_b': s(ks[3], (D_INNER,), 0.1), 'x_proj_w': s(ks[4], (DT_RANK + 2 * STATE, D_INNER)), 'dt_proj_w': s(ks[5], (D_INNER, DT_RANK), 0.1), 'dt_proj_b': s(ks[6], (D_INNER,), 0.1), 'A_log': s(ks[7], (D_INNER, STATE), 0.5), 'out_proj_w': s(ks[8], (HIDDEN, D_INNER))}
    _L0_attn_in = _L0_attn_setup()

    def _L0_ffn_setup():
        import jax, jax.numpy as jnp
        from jax import lax
        import numpy as np
        D = 256
        N = 8
        K = 2
        KS = 1
        H = 2 * D
        B, S = (2, 256)

        def _moe(x_BSD, Wg_DN, Wl1_ND2H, Wl2_NHD):
            b, s, d = x_BSD.shape
            x_MD = x_BSD.reshape(b * s, d)
            Nr = N - KS
            s_raw_MN = x_MD @ Wg_DN
            routed = jax.nn.softmax(s_raw_MN[:, :Nr].astype(jnp.float32), axis=-1)
            shared = jax.nn.softmax(s_raw_MN[:, Nr:].astype(jnp.float32), axis=-1)
            _, idx_MK = lax.top_k(routed, K - KS)
            mask = jnp.sum(jax.nn.one_hot(idx_MK, Nr, dtype=jnp.float32), axis=1)
            sel = routed * mask
            routed_n = sel / jnp.sum(sel, axis=-1, keepdims=True)
            shared_n = shared / jnp.sum(shared, axis=-1, keepdims=True)
            gates_MN = jnp.concatenate([routed_n, shared_n], axis=-1).astype(x_MD.dtype)

            def step(y_MD, inp):
                w1_D2H, w2_HD, g_M = inp
                z = x_MD @ w1_D2H
                a, bgate = jnp.split(z, 2, axis=-1)
                h = jax.nn.silu(bgate) * a
                return (y_MD + g_M[:, None] * (h @ w2_HD), None)
            y0 = jnp.zeros_like(x_MD)
            y_MD, _ = lax.scan(step, y0, (Wl1_ND2H, Wl2_NHD, gates_MN.T))
            return y_MD.reshape(b, s, d)
        key = jax.random.key(seed)
        k1, k2, k3, k4 = jax.random.split(key, 4)
        scale = 1.0 / np.sqrt(D).astype(np.float32)
        x = jax.random.normal(k1, (B, S, D), dtype=jnp.float32)
        Wg = jax.random.normal(k2, (D, N), dtype=jnp.float32) * scale
        Wl1 = jax.random.normal(k3, (N, D, 2 * H), dtype=jnp.float32) * scale
        Wl2 = jax.random.normal(k4, (N, H, D), dtype=jnp.float32) * scale
        return {'x_BSD': x, 'Wg_DN': Wg, 'Wl1_ND2H': Wl1, 'Wl2_NHD': Wl2}
    _L0_ffn_in = _L0_ffn_setup()
    _L0_c = _w((lambda *s: np.random.randn(*s).astype(np.float32) * 0.05)(4, 256))
    _L0_wmod = _w((lambda *s: np.random.randn(*s).astype(np.float32) * 0.05)(256, 6 * 256) * 256 ** (-0.5))
    _d = {'L0_attn_x': _L0_attn_in['x'], 'L0_attn_in_proj_w': _L0_attn_in['in_proj_w'], 'L0_attn_conv_w': _L0_attn_in['conv_w'], 'L0_attn_conv_b': _L0_attn_in['conv_b'], 'L0_attn_x_proj_w': _L0_attn_in['x_proj_w'], 'L0_attn_dt_proj_w': _L0_attn_in['dt_proj_w'], 'L0_attn_dt_proj_b': _L0_attn_in['dt_proj_b'], 'L0_attn_A_log': _L0_attn_in['A_log'], 'L0_attn_out_proj_w': _L0_attn_in['out_proj_w'], 'L0_ffn_Wg_DN': _L0_ffn_in['Wg_DN'], 'L0_ffn_Wl1_ND2H': _L0_ffn_in['Wl1_ND2H'], 'L0_ffn_Wl2_NHD': _L0_ffn_in['Wl2_NHD'], 'L0_c': _L0_c, 'L0_wmod': _L0_wmod}
    _x0 = _d['L0_attn_x']
    _d['L0_attn_x'] = jax.random.normal(jax.random.fold_in(jax.random.key(seed), 1), (4, 2048, 256), dtype=_x0.dtype)
    del _x0
    return _d

def reference(L0_attn_x, L0_attn_in_proj_w, L0_attn_conv_w, L0_attn_conv_b, L0_attn_x_proj_w, L0_attn_dt_proj_w, L0_attn_dt_proj_b, L0_attn_A_log, L0_attn_out_proj_w, L0_ffn_Wg_DN, L0_ffn_Wl1_ND2H, L0_ffn_Wl2_NHD, L0_c, L0_wmod):

    def _L0_attn_ref(x, in_proj_w, conv_w, conv_b, x_proj_w, dt_proj_w, dt_proj_b, A_log, out_proj_w):
        import jax, jax.numpy as jnp
        import numpy as np
        HIDDEN = 256
        D_INNER = 512
        DT_RANK = 64
        STATE = 16
        KCONV = 4

        def _selective_scan(u, delta, A, B, C):
            deltaA = jnp.exp(delta[..., None] * A)
            dBu = (delta * u)[..., None] * B[:, :, None, :]
            deltaA_t = jnp.moveaxis(deltaA, 1, 0)
            dBu_t = jnp.moveaxis(dBu, 1, 0)
            C_t = jnp.moveaxis(C, 1, 0)

            def step(h, inp):
                dA_i, dBu_i, C_i = inp
                h = dA_i * h + dBu_i
                y = jnp.einsum('bdn,bn->bd', h, C_i)
                return (h, y)
            h0 = jnp.zeros(u.shape[:1] + u.shape[2:] + (A.shape[1],), dtype=u.dtype)
            _, ys = jax.lax.scan(step, h0, (deltaA_t, dBu_t, C_t))
            return jnp.moveaxis(ys, 0, 1)
        b, l, _ = x.shape
        xr = x @ in_proj_w.T
        xs, res = jnp.split(xr, 2, axis=-1)
        xc = jnp.moveaxis(xs, 1, 2)
        xc = jax.lax.conv_general_dilated(xc, conv_w, window_strides=(1,), padding=[(KCONV - 1, 0)], feature_group_count=D_INNER, dimension_numbers=('NCH', 'OIH', 'NCH'))
        xc = xc + conv_b[None, :, None]
        xs = jnp.moveaxis(xc, 2, 1)
        xs = jax.nn.silu(xs)
        x_dbl = xs @ x_proj_w.T
        dt, B, C = jnp.split(x_dbl, [DT_RANK, DT_RANK + STATE], axis=-1)
        delta = jax.nn.softplus(dt @ dt_proj_w.T + dt_proj_b)
        A = -jnp.exp(A_log.astype(jnp.float32))
        y = _selective_scan(xs, delta, A, B, C)
        y = y * jax.nn.silu(res)
        return y @ out_proj_w.T

    def _L0_ffn_ref(x_BSD, Wg_DN, Wl1_ND2H, Wl2_NHD):
        import jax, jax.numpy as jnp
        from jax import lax
        import numpy as np
        D = 256
        N = 8
        K = 2
        KS = 1
        H = 2 * D
        B, S = (2, 256)

        def _moe(x_BSD, Wg_DN, Wl1_ND2H, Wl2_NHD):
            b, s, d = x_BSD.shape
            x_MD = x_BSD.reshape(b * s, d)
            Nr = N - KS
            s_raw_MN = x_MD @ Wg_DN
            routed = jax.nn.softmax(s_raw_MN[:, :Nr].astype(jnp.float32), axis=-1)
            shared = jax.nn.softmax(s_raw_MN[:, Nr:].astype(jnp.float32), axis=-1)
            _, idx_MK = lax.top_k(routed, K - KS)
            mask = jnp.sum(jax.nn.one_hot(idx_MK, Nr, dtype=jnp.float32), axis=1)
            sel = routed * mask
            routed_n = sel / jnp.sum(sel, axis=-1, keepdims=True)
            shared_n = shared / jnp.sum(shared, axis=-1, keepdims=True)
            gates_MN = jnp.concatenate([routed_n, shared_n], axis=-1).astype(x_MD.dtype)

            def step(y_MD, inp):
                w1_D2H, w2_HD, g_M = inp
                z = x_MD @ w1_D2H
                a, bgate = jnp.split(z, 2, axis=-1)
                h = jax.nn.silu(bgate) * a
                return (y_MD + g_M[:, None] * (h @ w2_HD), None)
            y0 = jnp.zeros_like(x_MD)
            y_MD, _ = lax.scan(step, y0, (Wl1_ND2H, Wl2_NHD, gates_MN.T))
            return y_MD.reshape(b, s, d)
        return _moe(x_BSD, Wg_DN, Wl1_ND2H, Wl2_NHD)
    x = L0_attn_x
    mod = (_silu(L0_c) @ L0_wmod).reshape(L0_c.shape[0], 6, 1, -1)
    sa, ca, ga, sb, cb, gb = (mod[:, 0], mod[:, 1], mod[:, 2], mod[:, 3], mod[:, 4], mod[:, 5])
    ga = (2 * (ga >= 0) - 1) * jnp.maximum(jnp.abs(ga), 0.25)
    gb = (2 * (gb >= 0) - 1) * jnp.maximum(jnp.abs(gb), 0.25)
    h = _layernorm(x, axis=-1) * (1 + ca) + sa
    x = x + ga * _L0_attn_ref(h, L0_attn_in_proj_w, L0_attn_conv_w, L0_attn_conv_b, L0_attn_x_proj_w, L0_attn_dt_proj_w, L0_attn_dt_proj_b, L0_attn_A_log, L0_attn_out_proj_w)
    h = _layernorm(x, axis=-1) * (1 + cb) + sb
    x = x + gb * _L0_ffn_ref(h, L0_ffn_Wg_DN, L0_ffn_Wl1_ND2H, L0_ffn_Wl2_NHD)
    return x

_drawn_inputs = setup_inputs


def setup_inputs(seed=0):
    import zlib

    import numpy as np

    out = dict(_drawn_inputs(seed))
    spreads = {}
    factors = {}
    for name, (base, spread) in spreads.items():
        noise = np.random.default_rng([zlib.crc32(name.encode()), seed]).standard_normal(out[name].shape)
        drawn = base * np.exp(spread * noise) if base else spread * noise
        out[name] = jnp.asarray(drawn.astype(out[name].dtype))
    for name, factor in factors.items():
        out[name] = (out[name] * factor).astype(out[name].dtype)
    return out
```

```python
from contextlib import ExitStack

import concourse.bass as bass
from concourse import mybir

F32 = mybir.dt.float32
I32 = mybir.dt.int32
ALU = mybir.AluOpType
ACT = mybir.ActivationFunctionType
AX_X = mybir.AxisListType.X

P = 128
BATCH, SEQ, D = 4, 2048, 256
DI, DT_RANK, STATE, KCONV = 512, 64, 16, 4
NEXP, H = 8, 512
NR = NEXP - 1
T = 512
NCHUNK = BATCH * SEQ // T
CPB = SEQ // T
TT = T // P
KD = D // P
KI = DI // P
DS = 32
NSET = DI // DS
NF = P // DS
NG = STATE // NF
SPC = P // DS
RING = 8
NBANK = 3
EPS = 1e-5
BIG = 3.4028234e38
NTILE = BATCH * SEQ // P
SLOT_TILES = NTILE + NR - 1
PROJ = DT_RANK + 2 * STATE
EMPTY = 1 << 20


def hold(eng, sem, value, held):
    eng.wait_ge(sem, value)
    eng.sem_inc(held, 1)


def setup_program(nc, ins, t, mod2_dram, gb_dram):
    with ExitStack() as ctx:
        sem = lambda n: ctx.enter_context(nc.semaphore(n))
        cT = ctx.enter_context(nc.sbuf_tensor("cT", [P, KD, BATCH], F32))
        cs = ctx.enter_context(nc.sbuf_tensor("cs", [P, KD, BATCH], F32))
        csb = ctx.enter_context(nc.sbuf_tensor("csb", [P, BATCH, KD, P], F32))
        wmod = ctx.enter_context(nc.sbuf_tensor("wmod", [P, KD, 6 * D], F32))
        rows = ctx.enter_context(nc.sbuf_tensor("rows", [P, 4, D], F32))
        mod2 = ctx.enter_context(nc.sbuf_tensor("mod2", [P, 3, BATCH, D], F32))
        pos = ctx.enter_context(nc.sbuf_tensor("posm", [P, 2, D], F32))
        pc = ctx.enter_context(nc.psum_tensor("pc", [P, 2 * KD, BATCH], F32))
        pr = ctx.enter_context(nc.psum_tensor("pr", [P, 2, 2, D], F32))
        c_loaded, zeroed, selectors = sem("c_loaded"), sem("zeroed"), sem("selectors")
        w_loaded, c_silu, c_spread = sem("w_loaded"), sem("c_silu"), sem("c_spread")
        cols_ready, cols_kept, row_ready, row_kept = sem("cols_ready"), sem("cols_kept"), sem("row_ready"), sem("row_kept")
        rows_step, a_loaded, a_exp, mod2_stored = sem("rows_step"), sem("a_loaded"), sem("a_exp"), sem("mod2_stored")
        block = ctx.enter_context(nc.Block())

        @block.sync
        def _(sp):
            sp.dma_start(cT[:], ins["c"]).then_inc(c_loaded, 16)
            sp.dma_start(wmod[:], ins["wmod"].rearrange("(k p) n -> p k n", p=P)).then_inc(c_loaded, 16)
            sp.dma_start(t["a"][:], ins["a_cols"]).then_inc(a_loaded, 16)
            sp.dma_start(t["cw"][:], ins["conv_w"]).then_inc(w_loaded, 16)
            sp.dma_start(t["cb"][:], ins["conv_b"]).then_inc(w_loaded, 16)
            sp.dma_start(t["dtb"][:], ins["dt_b"]).then_inc(w_loaded, 16)
            sp.dma_start(t["w_in"][:], ins["w_in"].rearrange("(k p) n -> p k n", p=P)).then_inc(w_loaded, 16)
            sp.dma_start(t["w_x"][:], ins["w_x"].rearrange("(k p) n -> p k n", p=P)).then_inc(w_loaded, 16)
            sp.dma_start(t["w_dt"][:], ins["w_dt"]).then_inc(w_loaded, 16)
            sp.dma_start(t["w_out"][:], ins["w_out"].rearrange("(k p) n -> p k n", p=P)).then_inc(w_loaded, 16)
            sp.wait_ge(w_loaded, 7 * 16)
            sp.wait_ge(rows_step, 5 * BATCH)
            sp.dma_start(mod2_dram, mod2[:]).then_inc(mod2_stored, 16)
            sp.dma_start(gb_dram.rearrange("(o b) d -> o b d", o=1), mod2[0:1, 2]).then_inc(mod2_stored, 16)
            sp.wait_ge(mod2_stored, 32)

        @block.gpsimd
        def _(pool):
            nc.gpsimd.memset(t["ident"][:], 0.0).then_inc(zeroed, 1)
            nc.gpsimd.memset(t["spread"][:], 0.0).then_inc(zeroed, 1)
            nc.gpsimd.memset(t["gather"][:], 0.0).then_inc(zeroed, 1)
            nc.gpsimd.memset(t["limits"][:, :, 0], BIG).then_inc(zeroed, 1)
            nc.gpsimd.memset(t["limits"][:, :, 1], -BIG).then_inc(zeroed, 1)
            nc.gpsimd.memset(t["mhalf"][:], -0.5).then_inc(zeroed, 1)
            nc.gpsimd.memset(t["state"][:], 0.0).then_inc(zeroed, 1)
            nc.gpsimd.memset(t["xpad"][:, :, 0:KCONV - 1], 0.0).then_inc(zeroed, 1)
            pool.wait_ge(zeroed, 8)
            nc.gpsimd.affine_select(out=t["ident"][:], in_=t["ident"][:], compare_op=ALU.not_equal, fill=1.0,
                                    base=0, pattern=[[-1, P]], channel_multiplier=1).then_inc(selectors, 1)
            sv = t["spread"][:].rearrange("p q (a d) -> p q a d", d=DS)
            nc.gpsimd.affine_select(out=sv, in_=sv, compare_op=ALU.not_equal, fill=1.0, base=0,
                                    pattern=[[-DS, SPC], [0, NF], [-1, DS]], channel_multiplier=1).then_inc(selectors, 1)
            nc.gpsimd.memset(t["limits"][:, 0:NCHUNK + 1:CPB, :], 0.0).then_inc(selectors, 1)
            for a in range(NF):
                nc.gpsimd.affine_select(out=t["gather"][:], in_=t["gather"][:], compare_op=ALU.not_equal, fill=1.0,
                                        base=-DS * a, pattern=[[-1, DS]], channel_multiplier=1).then_inc(selectors, 1)
                pool.wait_ge(selectors, 4 + a)

        @block.scalar
        def _(act):
            act.wait_ge(c_loaded, 2 * 16)
            nc.scalar.activation(cs[:], cT[:], ACT.Silu).then_inc(c_silu, 1)
            act.wait_ge(a_loaded, 16)
            nc.scalar.activation(t["a"][:], t["a"][:], ACT.Exp).then_inc(a_exp, 1)

        @block.vector
        def _(dve):
            dve.wait_ge(c_silu, 1)
            for b in range(BATCH):
                for kc in range(KD):
                    last = nc.vector.tensor_copy(csb[:, b, kc, :], cs[:, kc, b:b + 1].to_broadcast([P, P]))
            last.then_inc(c_spread, 1)
            dve.wait_ge(a_exp, 1)
            nc.vector.tensor_scalar(t["a"][:], t["a"][:], -1.0, None, ALU.mult)
            dve.wait_ge(selectors, 1)
            dve.wait_ge(w_loaded, 7 * 16)
            for j in range(KI):
                for k in range(KCONV):
                    nc.vector.tensor_scalar(t["w_conv"][:, j, k, :], t["ident"][:], t["cw"][:, j, k:k + 1], None, ALU.mult)
            dve.wait_ge(cols_ready, 1)
            nc.vector.tensor_copy(t["sa"][:], pc[:, 0:KD, :])
            nc.vector.tensor_scalar(t["ca"][:], pc[:, KD:2 * KD, :], 1.0, None, ALU.add).then_inc(cols_kept, 1)
            step = 0
            for b in range(BATCH):
                dve.wait_ge(row_ready, b + 1)
                nc.vector.tensor_copy(rows[:, 0:2, :], pr[:, 0, :, :]).then_inc(rows_step, 1)
                nc.vector.tensor_copy(mod2[:, 1, b, :], pr[:, 1, 0, :])
                nc.vector.tensor_scalar(mod2[:, 0, b, :], pr[:, 1, 1, :], 1.0, None, ALU.add).then_inc(row_kept, 1)
                dve.wait_ge(rows_step, step + 1)
                nc.vector.tensor_scalar(pos[:], rows[:, 0:2, :], 0.0, None, ALU.is_ge)
                nc.vector.tensor_scalar(rows[:, 2:4, :], rows[:, 0:2, :], -1.0, None, ALU.mult).then_inc(rows_step, 1)
                dve.wait_ge(rows_step, step + 2)
                nc.vector.tensor_tensor(rows[:, 2:4, :], rows[:, 2:4, :], rows[:, 0:2, :], ALU.max)
                nc.vector.tensor_scalar(pos[:], pos[:], 2.0, -1.0, ALU.mult, ALU.add).then_inc(rows_step, 1)
                dve.wait_ge(rows_step, step + 3)
                nc.vector.tensor_scalar(rows[:, 2:4, :], rows[:, 2:4, :], 0.25, None, ALU.max).then_inc(rows_step, 1)
                dve.wait_ge(rows_step, step + 4)
                nc.vector.tensor_tensor(t["ga"][:, b, :], rows[:, 2, :], pos[:, 0, :], ALU.mult)
                nc.vector.tensor_tensor(mod2[:, 2, b, :], rows[:, 3, :], pos[:, 1, :], ALU.mult).then_inc(rows_step, 1)
                step += 5
                dve.wait_ge(rows_step, step)

        @block.tensor
        def _(pe):
            pe.wait_ge(c_loaded, 2 * 16)
            pe.wait_ge(c_silu, 1)
            for n in range(2 * KD):
                for kc in range(KD):
                    last = nc.tensor.matmul(pc[:, n, :], wmod[:, kc, n * P:(n + 1) * P], cs[:, kc, :],
                                            start=(kc == 0), stop=(kc == KD - 1))
            last.then_inc(cols_ready, 1)
            pe.wait_ge(c_spread, 1)
            for b in range(BATCH):
                if b:
                    pe.wait_ge(row_kept, b)
                for n, part in enumerate((2, 5, 3, 4)):
                    for kc in range(KD):
                        last = nc.tensor.matmul(pr[:, n // 2, n % 2, :], csb[:, b, kc, :], wmod[:, kc, part * D:(part + 1) * D],
                                                start=(kc == 0), stop=(kc == KD - 1))
                last.then_inc(row_ready, 1)


def mamba_program(nc, ins, t, bc_dram, x1_dram):
    x_in = ins["x"].rearrange("(c t p) d -> c p t d", t=TT, p=P)
    x1_out = x1_dram.rearrange("(c t p) d -> c p t d", t=TT, p=P)
    with ExitStack() as ctx:
        sem = lambda n: ctx.enter_context(nc.semaphore(n))
        sb = lambda n, s: ctx.enter_context(nc.sbuf_tensor(n, s, F32))
        ps = lambda n, s: ctx.enter_context(nc.psum_tensor(n, s, F32))
        xin = sb("xin", [P, TT, D])
        hT = xin[:].rearrange("p t d -> p (t d)").rearrange("p (k t) -> p k t", k=KD)
        stats, mv, var, rstd = sb("stats", [P, TT, 6]), sb("mv", [P, TT, 2]), sb("var", [P, TT]), sb("rstd", [P, TT])
        xpad, us = t["xpad"], sb("us", [P, KI, T])
        res = sb("res", [P, 2, KI, T])
        xdbl = sb("xdbl", [PROJ, T])
        delta, du, relu = sb("delta", [P, KI, T]), sb("du", [P, KI, T]), sb("relu", [P, 2, T])
        b_rep, c_rep = sb("b_rep", [P, 2, NG * T]), sb("c_rep", [P, 2, NG * T])
        dbu, hs = sb("dbu", [P, 2, NG, T]), sb("hs", [P, RING, NG, T])
        xres, gy = sb("xres", [P, TT, D]), sb("gy", [P, 2, D])
        state, bound = t["state"], sb("bound", [P, 2])
        banks = [ps(f"bank{i}", [P, T]) for i in range(NBANK)]
        d_rep, u_rep, y_ps = ps("d_rep", [P, T]), ps("u_rep", [P, T]), ps("y_ps", [P, T])
        dA = ps("dA", [P, 2, T])

        x_loaded, var_ready, rstd_ready, xn_ready = sem("x_loaded"), sem("var_ready"), sem("rstd_ready"), sem("xn_ready")
        ln_step, hT_ready = sem("ln_step"), sem("hT_ready")
        turned, xs_made, res_made, conv_made = sem("turned"), sem("xs_made"), sem("res_made"), sem("conv_made")
        xdbl_made, dt_made, out_made = sem("xdbl_made"), sem("dt_made"), sem("out_made")
        halo_ready = sem("halo_ready")
        xs_ready, us_pre, us_ready, res_pre, res_ready = sem("xs_ready"), sem("us_pre"), sem("us_ready"), sem("res_pre"), sem("res_ready")
        xdbl_ready, bc_kept, bc_loaded = sem("xdbl_ready"), sem("bc_kept"), sem("bc_loaded")
        sp_step, relu_ready, log_ready, delta_ready, du_ready = sem("sp_step"), sem("relu_ready"), sem("log_ready"), sem("delta_ready"), sem("du_ready")
        drep_ready, urep_ready, da_ready = sem("drep_ready"), sem("urep_ready"), sem("da_ready")
        dbu_done, scan_done, state_saved, hc_ready = sem("dbu_done"), sem("scan_done"), sem("state_saved"), sem("hc_ready")
        y_ready, yg_ready, gy_ready = sem("y_ready"), sem("yg_ready"), sem("gy_ready")
        held, bound_set = sem("held"), sem("bound_set")
        xres_loaded, x1_ready, x1_stored = sem("xres_loaded"), sem("x1_ready"), sem("x1_stored")
        block = ctx.enter_context(nc.Block())

        front = ([("T", k) for k in range(KD)] + [("XS", 0), ("XS", 1), ("XS", 2), ("XS", 3), ("RS", 0), ("RS", 1), ("CV", 0),
                 ("RS", 2), ("CV", 1), ("CV", 2), ("RS", 3), ("CV", 3), ("XP", 0)] + [("DT", j) for j in range(KI)])
        back = [("OP", 0), ("OP", 1)]
        bank_of = {g: i % NBANK for i, g in enumerate(front)} | {g: i + 1 for i, g in enumerate(back)}
        plan = {2: [("T", 0), ("T", 1)], 3: [("XS", 0), ("XS", 1)], 4: [("OP", 0), ("OP", 1)], 5: [("XS", 2)],
                6: [("XS", 3), ("RS", 0)], 7: [("RS", 1), ("CV", 0)], 8: [("RS", 2), ("CV", 1)], 9: [("CV", 2)],
                10: [("RS", 3), ("CV", 3)], 12: [("XP", 0)], 13: [("DT", 0)], 14: [("DT", 1), ("DT", 2)], 15: [("DT", 3)]}
        order = [g for s in range(NSET) for g in plan.get(s, [])]
        SILU_AT = 11
        DELTAS_AT = {13: [0], 14: [1, 2], 15: [3]}
        made = {"T": turned, "XS": xs_made, "RS": res_made, "CV": conv_made, "XP": xdbl_made, "DT": dt_made, "OP": out_made}
        kept = {"T": hT_ready, "XS": xs_ready, "RS": res_pre, "CV": us_pre, "XP": xdbl_ready, "DT": relu_ready, "OP": gy_ready}
        many = {"T": KD, "XS": KI, "RS": KI, "CV": KI, "XP": 1, "DT": KI, "OP": 2}

        def chunk_of(g, c):
            return 0 if c is None else c + 1 if g in front else c - 1

        def count(g, c):
            return many[g[0]] * chunk_of(g, c) + g[1] + 1

        def take_bank(pe, g, c):
            same = lambda x: bank_of[x] == bank_of[g]
            is_there = lambda x, b: x in front if isinstance(b, int) and b == 0 else x in back if isinstance(b, int) and b >= NCHUNK - 1 else True
            if c is None:
                before = [(x, None) for x in front[:front.index(g)] if same(x)]
            else:
                ahead = back[:back.index(g)] if isinstance(c, int) and c == NCHUNK else order[:order.index(g)]
                before = [(x, c) for x in ahead if same(x) and is_there(x, c)]
                if not before:
                    earlier = c - 1 if not (isinstance(c, int) and c == 0) else None
                    seq = front if earlier is None else order
                    before = [(x, earlier) for x in seq if same(x) and (earlier is None or is_there(x, earlier))]
                    if not before:
                        before = [(x, c - 2) for x in order if same(x)]
            if before:
                x, b = before[-1]
                pe.wait_ge(kept[x[0]], count(x, b))
            return banks[bank_of[g]]

        def read_bank(eng, g, c):
            eng.wait_ge(made[g[0]], count(g, c))
            return banks[bank_of[g]]

        def bodies(eng, body):
            body(0, 0, False, True)
            with eng.Fori(1, NCHUNK - 2, 2) as c:
                body(c, 1, True, True)
                body(c + 1, 0, True, True)
            body(NCHUNK - 1, 1, True, False)

        @block.sync
        def _(sp):
            def load_x(f):
                sp.dma_start(xin[:], x_in[f]).then_inc(x_loaded, 16)

            def spread_bc(f, par):
                sp.wait_ge(xdbl_ready, f + 1)
                sp.dma_start(bc_dram, xdbl[DT_RANK:PROJ, :]).then_inc(bc_kept, 16)
                hold(sp, bc_kept, 16 * f + 16, held)
                if not isinstance(f, int) or f >= 2:
                    sp.wait_ge(dbu_done, NSET * (f - 1))
                    sp.wait_ge(hc_ready, NSET * (f - 1))
                for n, rep in enumerate((b_rep, c_rep)):
                    for nf in range(NF):
                        r = n * STATE + nf * NG
                        sp.dma_start(rep[DS * nf:DS * nf + DS, par, :],
                                     bc_dram[r:r + NG, :].rearrange("n t -> (n t)").partition_broadcast(DS)).then_inc(bc_loaded, 16)

            def body(c, par, back_, front_):
                if back_:
                    if not isinstance(c, int) or c > 1:
                        hold(sp, x1_stored, 16 * (c - 1), held)
                    sp.dma_start(xres[:], x_in[c - 1]).then_inc(xres_loaded, 16)
                if front_:
                    hold(sp, res_made, KI * (c + 2), held)
                    sp.dma_start(xin[:], x_pad(c)).then_inc(x_loaded, 16)
                if back_:
                    hold(sp, x1_ready, 2 * c, held)
                    sp.dma_start(x1_out[c - 1], xres[:]).then_inc(x1_stored, 16)
                if front_:
                    spread_bc(c + 1, 1 - par)

            def x_pad(c):
                return x_in[c + 2] if not (isinstance(c, int) and c + 2 >= NCHUNK) else x_in[NCHUNK - 1]

            load_x(0)
            sp.wait_ge(res_made, KI)
            load_x(1)
            spread_bc(0, 0)
            body(0, 0, False, True)
            with sp.Fori(1, NCHUNK - 4, 2) as c:
                body(c, 1, True, True)
                body(c + 1, 0, True, True)
            body(NCHUNK - 3, 1, True, True)
            c = NCHUNK - 2
            sp.wait_ge(x1_stored, 16 * (c - 1))
            sp.dma_start(xres[:], x_in[c - 1]).then_inc(xres_loaded, 16)
            sp.wait_ge(x1_ready, 2 * c)
            sp.dma_start(x1_out[c - 1], xres[:]).then_inc(x1_stored, 16)
            spread_bc(c + 1, 1)
            body(NCHUNK - 1, 1, True, False)
            body(NCHUNK, 0, True, False)
            sp.wait_ge(x1_stored, 16 * NCHUNK)

        @block.tensor
        def _(pe):
            def group(g, c, f, par=0):
                kind, j = g
                ps_ = take_bank(pe, g, c)
                if kind == "T":
                    if j == 0:
                        pe.wait_ge(xn_ready, f + 1)
                    for tt in range(TT):
                        last = nc.tensor.transpose(ps_[:, tt * P:(tt + 1) * P], xin[:, tt, j * P:(j + 1) * P], t["ident"][:])
                elif kind in ("XS", "RS"):
                    col = j * P + (DI if kind == "RS" else 0)
                    pe.wait_ge(hT_ready, KD * f + KD)
                    for k in range(KD):
                        last = nc.tensor.matmul(ps_[:, :], t["w_in"][:, k, col:col + P], hT[:, k, :], start=(k == 0), stop=(k == KD - 1))
                elif kind == "CV":
                    pe.wait_ge(xs_ready, KI * f + j + 1)
                    for k in range(KCONV):
                        last = nc.tensor.matmul(ps_[:, :], t["w_conv"][:, j, k, :], xpad[:, j, k:k + T], start=(k == 0), stop=(k == KCONV - 1))
                elif kind == "XP":
                    pe.wait_ge(us_ready, f + 1)
                    for k in range(KI):
                        last = nc.tensor.matmul(ps_[0:PROJ, :], t["w_x"][:, k, :], us[:, k, :], start=(k == 0), stop=(k == KI - 1))
                elif kind == "DT":
                    pe.wait_ge(xdbl_ready, f + 1)
                    last = nc.tensor.matmul(ps_[:, :], t["w_dt"][:, j * P:(j + 1) * P], xdbl[0:DT_RANK, :], start=True, stop=True)
                elif kind == "OP":
                    pe.wait_ge(yg_ready, KI * c)
                    for h in range(2):
                        for k in range(KI):
                            tt = 2 * j + h
                            last = nc.tensor.matmul(ps_[:, h * D:(h + 1) * D], res[:, 1 - par, k, tt * P:(tt + 1) * P], t["w_out"][:, k, :],
                                                    start=(k == 0), stop=(k == KI - 1))
                last.then_inc(made[kind], 1)

            def spread(c, s):
                j, q = divmod(s, SPC)
                pe.wait_ge(delta_ready, KI * c + j + 1)
                if not (isinstance(c, int) and c == 0 and s == 0):
                    pe.wait_ge(da_ready, NG * (NSET * c + s))
                nc.tensor.matmul(d_rep[:], t["spread"][:, q, :], delta[:, j, :], start=True, stop=True).then_inc(drep_ready, 1)
                pe.wait_ge(du_ready, KI * c + j + 1)
                if not (isinstance(c, int) and c == 0 and s == 0):
                    pe.wait_ge(dbu_done, NSET * c + s)
                nc.tensor.matmul(u_rep[:], t["spread"][:, q, :], du[:, j, :], start=True, stop=True).then_inc(urep_ready, 1)

            def sum_states(c, j):
                pe.wait_ge(hc_ready, NSET * c + SPC * (j + 1))
                if not (isinstance(c, int) and c == 0 and j == 0):
                    pe.wait_ge(yg_ready, KI * c + j)
                for g in range(NG):
                    for q in range(SPC):
                        last = nc.tensor.matmul(y_ps[DS * q:DS * q + DS, :], t["gather"][:], hs[:, (SPC * j + q) % RING, g, :],
                                                start=(g == 0), stop=(g == NG - 1), skip_group_check=True,
                                                tile_position=(0, DS * q))
                last.then_inc(y_ready, 1)

            def body(c, par, back_, front_):
                for s in range(NSET):
                    spread(c, s)
                    if s == 1 and back_:
                        sum_states(c - 1, KI - 1)
                    if s > SPC and s % SPC == 1:
                        sum_states(c, s // SPC - 1)
                    for g in plan.get(s, []):
                        if front_ if g in front else back_:
                            group(g, c, c + 1, par)

            for g in front:
                group(g, None, 0)
            bodies(pe, body)
            sum_states(NCHUNK - 1, KI - 1)
            for g in back:
                group(g, NCHUNK, None, 0)

        @block.scalar
        def _(act):
            def group(g, c, f, half, first=False):
                kind, j = g
                if kind == "OP":
                    return
                ps_ = read_bank(act, g, c)
                b = f // CPB
                if kind == "T":
                    if j == 0:
                        act.wait_ge(turned, KD * (f + 1))
                    nc.scalar.activation(hT[:, j, :], ps_[:, :], ACT.Identity, scale=t["ca"][:, j, bass.ds(b, 1)],
                                         bias=t["sa"][:, j, bass.ds(b, 1)]).then_inc(hT_ready, 1)
                elif kind == "XS":
                    if j == 0 and not first:
                        act.wait_ge(halo_ready, f)
                    nc.scalar.activation(xpad[:, j, KCONV - 1:], ps_[:, :], ACT.Copy).then_inc(xs_ready, 1)
                elif kind == "RS":
                    if j == 0 and not first and not (isinstance(f, int) and f == 1):
                        act.wait_ge(out_made, 2 * (f - 1))
                    nc.scalar.activation(res[:, half, j, :], ps_[:, :], ACT.Copy).then_inc(res_pre, 1)
                elif kind == "CV":
                    if j == 0 and not first:
                        act.wait_ge(du_ready, KI * f)
                        act.wait_ge(xdbl_ready, f)
                    nc.scalar.activation(us[:, j, :], ps_[:, :], ACT.Identity, bias=t["cb"][:, j:j + 1]).then_inc(us_pre, 1)
                elif kind == "XP":
                    if not first:
                        act.wait_ge(dt_made, KI * f)
                        act.wait_ge(bc_kept, 16 * f)
                    nc.scalar.activation(xdbl[:, :], ps_[0:PROJ, :], ACT.Copy).then_inc(xdbl_ready, 1)
                elif kind == "DT":
                    n = KI * f + j
                    if not first:
                        act.wait_ge(urep_ready, NSET * (f - 1) + SPC * (j + 1))
                        act.wait_ge(drep_ready, NSET * (f - 1) + SPC * (j + 1))
                    nc.scalar.activation(delta[:, j, :], ps_[:, :], ACT.Abs, bias=t["dtb"][:, j:j + 1]).then_inc(sp_step, 1)
                    if not (first and j < 2):
                        act.wait_ge(delta_ready, n - 1)
                    nc.scalar.activation(relu[:, j % 2, :], ps_[:, :], ACT.Relu, bias=t["dtb"][:, j:j + 1]).then_inc(relu_ready, 1)
                    act.wait_ge(sp_step, 2 * n + 1)
                    nc.scalar.activation(delta[:, j, :], delta[:, j, :], ACT.Exp, scale=-1.0).then_inc(sp_step, 1)
                    act.wait_ge(sp_step, 2 * n + 2)
                    nc.scalar.activation(delta[:, j, :], delta[:, j, :], ACT.Ln, bias=1.0).then_inc(log_ready, 1)

            def silus(f, half):
                act.wait_ge(us_pre, KI * f + KI)
                nc.scalar.activation(us[:], us[:], ACT.Silu).then_inc(us_ready, 1)
                act.wait_ge(res_pre, KI * f + KI)
                nc.scalar.activation(res[:, half], res[:, half], ACT.Silu).then_inc(res_ready, 1)

            def exps(c, s):
                act.wait_ge(drep_ready, NSET * c + s + 1)
                for g in range(NG):
                    u = NG * s + g
                    if not (isinstance(c, int) and c == 0 and u < 2):
                        act.wait_ge(scan_done, NG * NSET * c + u - 1)
                    nc.scalar.activation(dA[:, u % 2, :], d_rep[:], ACT.Exp, scale=t["a"][:, u:u + 1]).then_inc(da_ready, 1)

            def body(c, par, back_, front_):
                for s in range(NSET):
                    exps(c, s)
                    if front_:
                        for g in plan.get(s, []):
                            group(g, c, c + 1, 1 - par)
                        if s == SILU_AT:
                            silus(c + 1, 1 - par)

            for g in front:
                if g == ("XP", 0):
                    silus(0, 0)
                group(g, None, 0, 0, first=True)
            bodies(act, body)

        @block.vector
        def _(dve):
            def layernorm(f, first=False):
                dve.wait_ge(x_loaded, 16 * f + 16)
                for tt in range(TT):
                    last = nc.vector.bn_stats(stats[:, tt, :], xin[:, tt, :])
                last.then_inc(ln_step, 1)
                hold(dve, ln_step, 2 * f + 1, held)
                for tt in range(TT):
                    last = nc.vector.bn_aggr(mv[:, tt, :], stats[:, tt, :])
                last.then_inc(ln_step, 1)
                dve.wait_ge(ln_step, 2 * f + 2)
                nc.vector.tensor_scalar(var[:], mv[:, :, 1], EPS, None, ALU.add).then_inc(var_ready, 1)

            def normalize(f):
                dve.wait_ge(rstd_ready, f + 1)
                for tt in range(TT):
                    last = nc.vector.tensor_scalar(xin[:, tt, :], xin[:, tt, :], mv[:, tt, 0:1], rstd[:, tt:tt + 1], ALU.subtract, ALU.mult)
                last.then_inc(xn_ready, 1)

            def halo(f):
                dve.wait_ge(conv_made, KI * f)
                nc.vector.tensor_scalar(xpad[:, :, 0:KCONV - 1], xpad[:, :, T:T + KCONV - 1], t["limits"][:, bass.ds(f, 1), 0],
                                        t["limits"][:, bass.ds(f, 1), 1], ALU.min, ALU.max).then_inc(halo_ready, 1)

            def deltas(f, j, first=False):
                n = KI * f + j
                dve.wait_ge(relu_ready, n + 1)
                dve.wait_ge(log_ready, n + 1)
                nc.vector.tensor_tensor(delta[:, j, :], delta[:, j, :], relu[:, j % 2, :], ALU.add).then_inc(delta_ready, 1)
                dve.wait_ge(delta_ready, n + 1)
                if j == 0:
                    dve.wait_ge(us_ready, f + 1)
                nc.vector.tensor_tensor(du[:, j, :], delta[:, j, :], us[:, j, :], ALU.mult).then_inc(du_ready, 1)

            def scan_set(c, s, par):
                n = NSET * c + s
                slot = s % RING
                dve.wait_ge(urep_ready, n + 1)
                if s == 0:
                    dve.wait_ge(bc_loaded, 16 * 2 * NF * (c + 1))
                if not (isinstance(c, int) and c == 0 and s < 2):
                    dve.wait_ge(scan_done, NG * (n - 1))
                nc.vector.tensor_tensor(dbu[:, s % 2, :, :], u_rep[:].unsqueeze(1).to_broadcast([P, NG, T]),
                                        b_rep[:, par, :].rearrange("p (g t) -> p g t", g=NG), ALU.mult).then_inc(dbu_done, 1)
                dve.wait_ge(dbu_done, n + 1)
                if s % SPC == 0:
                    j = s // SPC
                    if not (isinstance(c, int) and c == 0 and j < RING // SPC):
                        dve.wait_ge(y_ready, KI * c + j - RING // SPC + 1)
                if not (isinstance(c, int) and c == 0):
                    dve.wait_ge(state_saved, NSET * (c - 1) + s + 1)
                for g in range(NG):
                    u = NG * s + g
                    dve.wait_ge(da_ready, NG * n + g + 1)
                    nc.vector.tensor_tensor_scan(hs[:, slot, g, :], dA[:, u % 2, :], dbu[:, s % 2, g, :], state[:, u:u + 1],
                                                 ALU.mult, ALU.add).then_inc(scan_done, 1)

            def gate_y(c, j, half):
                dve.wait_ge(y_ready, KI * c + j + 1)
                if j == 0:
                    dve.wait_ge(res_ready, c + 1)
                nc.vector.tensor_tensor(res[:, half, j, :], y_ps[:], res[:, half, j, :], ALU.mult).then_inc(yg_ready, 1)

            def residual(c, j):
                g = ("OP", j)
                ps_ = read_bank(dve, g, c)
                if j == 0:
                    dve.wait_ge(xres_loaded, 16 * c)
                if not (isinstance(c, int) and c == 1 and j == 0):
                    dve.wait_ge(x1_ready, 2 * (c - 1) + j)
                nc.vector.tensor_tensor(gy[:], ps_[:].rearrange("p (h d) -> p h d", h=2),
                                        t["ga"][:, bass.ds((c - 1) // CPB, 1), :].to_broadcast([P, 2, D]), ALU.mult).then_inc(gy_ready, 1)
                dve.wait_ge(gy_ready, 2 * (c - 1) + j + 1)
                nc.vector.tensor_tensor(xres[:, 2 * j:2 * j + 2, :], xres[:, 2 * j:2 * j + 2, :], gy[:], ALU.add).then_inc(x1_ready, 1)

            def body(c, par, back_, front_):
                for s in range(NSET):
                    scan_set(c, s, par)
                    if front_:
                        if s == 0:
                            layernorm(c + 1)
                            halo(c + 1)
                        if s == 1:
                            normalize(c + 1)
                    if back_ and s == 2:
                        gate_y(c - 1, KI - 1, 1 - par)
                    if back_ and s == 5:
                        residual(c, 0)
                        residual(c, 1)
                    if s > SPC and s % SPC == 2:
                        gate_y(c, s // SPC - 1, par)
                    if front_:
                        for j in DELTAS_AT.get(s, []):
                            deltas(c + 1, j)

            layernorm(0)
            normalize(0)
            for j in range(KI):
                deltas(0, j)
            bodies(dve, body)
            gate_y(NCHUNK - 1, KI - 1, 1)
            residual(NCHUNK, 0)
            residual(NCHUNK, 1)

        @block.gpsimd
        def _(pool):
            def rsqrt(f):
                pool.wait_ge(var_ready, f + 1)
                nc.gpsimd.tensor_tensor(rstd[:], var[:], t["mhalf"][:, 0:TT], ALU.pow).then_inc(rstd_ready, 1)

            def body(c, par, back_, front_):
                if not (isinstance(c, int) and c == 0):
                    pool.wait_ge(state_saved, NSET * c)
                nc.gpsimd.tensor_copy(bound[:], t["limits"][:, c + 1, :]).then_inc(bound_set, 1)
                pool.wait_ge(bound_set, c + 1)
                for s in range(NSET):
                    n = NSET * c + s
                    slot = s % RING
                    hold(pool, scan_done, NG * (n + 1), held)
                    nc.gpsimd.tensor_scalar(state[:, NG * s:NG * s + NG], hs[:, slot, :, T - 1], bound[:, 0:1], bound[:, 1:2], ALU.min, ALU.max).then_inc(state_saved, 1)
                    if s == 0:
                        pool.wait_ge(bc_loaded, 16 * 2 * NF * (c + 1))
                    pool.wait_ge(state_saved, n + 1)
                    nc.gpsimd.tensor_tensor(hs[:, slot, :, :], hs[:, slot, :, :],
                                            c_rep[:, par, :].rearrange("p (g t) -> p g t", g=NG), ALU.mult).then_inc(hc_ready, 1)
                    if s == 0 and front_:
                        rsqrt(c + 1)

            rsqrt(0)
            bodies(pool, body)


def shared_program(nc, ins, t, mod2_dram, x1_dram, rows_dram, slots_dram):
    x1_in = x1_dram.rearrange("(c t p) d -> c p t d", t=TT, p=P)
    rows_out = rows_dram.rearrange("(c t p) (w d) -> w c p t d", t=TT, p=P, w=2)
    with ExitStack() as ctx:
        sem = lambda n: ctx.enter_context(nc.semaphore(n))
        sb = lambda n, s, dt=F32: ctx.enter_context(nc.sbuf_tensor(n, s, dt))
        ps = lambda n, s: ctx.enter_context(nc.psum_tensor(n, s, F32))
        mod2, wg = sb("mod2_sb", [P, 3, BATCH, D]), sb("wg_sb", [P, KD, NEXP])
        w1s, w2s = sb("w1s", [P, KD, 2 * H]), sb("w2s", [P, KI, D])
        x1, h2, h2T = sb("x1_sb", [P, 2, TT, D]), sb("h2", [P, 2, TT, D]), sb("h2T", [P, 2, KD, T])
        stats, mv, var, rstd = sb("stats2", [P, TT, 6]), sb("mv2", [P, TT, 2]), sb("var2", [P, TT]), sb("rstd2", [P, TT])
        gs = sb("gs", [P, 6, TT])
        sg, hid = sb("sg", [P, 2, T]), sb("hid", [P, KI, T])
        yg = sb("yg", [P, TT, D])
        empty = sb("empty", [P, SLOT_TILES, 2], I32)
        t_ps, a_ps, b_ps = ps("t_ps", [P, KD, T]), ps("a_ps", [P, 2, T]), ps("b_ps", [P, 2, T])
        y_ps, l_ps = ps("y2_ps", [P, 2, D]), ps("l_ps", [P, TT, NEXP])

        w_loaded, w_routed, x1_loaded = sem("w2_loaded"), sem("w_routed"), [sem("x1_loaded0"), sem("x1_loaded1")]
        held = sem("held3")
        empty_set, slots_set, ln_step, var_ready, rstd_ready = sem("empty_set"), sem("slots_set"), sem("ln2_step"), sem("var2_ready"), sem("rstd2_ready")
        h2_step, h2_ready, h2_stored = sem("h2_step"), sem("h2_ready"), [sem("h2_stored0"), sem("h2_stored1")]
        turned, h2T_ready, logits_made, logits_kept = sem("turned2"), sem("h2T_ready"), sem("logits_made"), sem("logits_kept")
        gate_step, gate_exp, gate_ready = sem("gate_step"), sem("gate_exp"), sem("gate_ready")
        z_made, silu_ready, hid_ready, y_made, y_used = sem("z_made"), sem("silu_ready"), sem("hid_ready"), sem("y_made"), sem("y_used")
        acc_ready, acc_stored = sem("acc_ready"), [sem("acc_stored0"), sem("acc_stored1")]
        block = ctx.enter_context(nc.Block())

        def bodies(eng, body):
            body(0, 0, 0, True)
            with eng.Fori(1, NCHUNK - 2, 2) as c:
                body(c, 1, (c - 1) // 2, True)
                body(c + 1, 0, (c + 1) // 2, True)
            body(NCHUNK - 1, 1, NCHUNK // 2 - 1, False)

        first = lambda c, n=1: isinstance(c, int) and c < n

        @block.sync
        def _(sp):
            def load(c, par):
                sp.dma_start(x1[:, par], x1_in[c]).then_inc(x1_loaded[par], 16)

            def body(c, par, k, more):
                if more:
                    if not first(c):
                        hold(sp, acc_stored[1 - par], 16 * ((c + 1) // 2), held)
                    load(c + 1, 1 - par)
                sp.wait_ge(h2_ready, c + 1)
                sp.dma_start(rows_out[0, c], h2[:, par]).then_inc(h2_stored[par], 16)
                sp.wait_ge(acc_ready, c + 1)
                sp.dma_start(rows_out[1, c], x1[:, par]).then_inc(acc_stored[par], 16)

            load(0, 0)
            sp.dma_start(mod2[:], mod2_dram).then_inc(w_loaded, 16)
            sp.dma_start(wg[:], ins["wg"].rearrange("(k p) n -> p k n", p=P)).then_inc(w_loaded, 16)
            sp.dma_start(w1s[:], ins["w1"][NEXP - 1].rearrange("(k p) n -> p k n", p=P)).then_inc(w_loaded, 16)
            sp.dma_start(w2s[:], ins["w2"][NEXP - 1].rearrange("(k p) n -> p k n", p=P)).then_inc(w_loaded, 16)
            bodies(sp, body)
            sp.wait_ge(empty_set, 2)
            sp.dma_start(slots_dram.rearrange("(p k) w -> p k w", p=P), empty[:]).then_inc(slots_set, 16)
            sp.wait_ge(slots_set, 16)
            for par in range(2):
                sp.wait_ge(h2_stored[par], 16 * NCHUNK // 2)
                sp.wait_ge(acc_stored[par], 16 * NCHUNK // 2)

        @block.gpsimd
        def _(pool):
            def rsqrt(c):
                pool.wait_ge(var_ready, c + 1)
                nc.gpsimd.tensor_tensor(rstd[:], var[:], t["mhalf"][:, 0:TT], ALU.pow).then_inc(rstd_ready, 1)

            nc.gpsimd.memset(empty[:, :, 0], EMPTY).then_inc(empty_set, 1)
            nc.gpsimd.memset(empty[:, :, 1], 0).then_inc(empty_set, 1)
            rsqrt(0)
            bodies(pool, lambda c, par, k, more: rsqrt(c + 1) if more else None)

        @block.tensor
        def _(pe):
            def turn(c, par):
                pe.wait_ge(h2_ready, c + 1)
                for k in range(KD):
                    if not first(c):
                        pe.wait_ge(h2T_ready, KD * (c - 1) + k + 1)
                    for tt in range(TT):
                        last = nc.tensor.transpose(t_ps[:, k, tt * P:(tt + 1) * P], h2[:, par, tt, k * P:(k + 1) * P], t["ident"][:])
                    last.then_inc(turned, 1)

            def logits(c, par):
                pe.wait_ge(h2T_ready, KD * (c + 1))
                if not first(c):
                    pe.wait_ge(logits_kept, c)
                for tt in range(TT):
                    for k in range(KD):
                        last = nc.tensor.matmul(l_ps[:, tt, :], h2T[:, par, k, tt * P:(tt + 1) * P], wg[:, k, :], start=(k == 0), stop=(k == KD - 1))
                last.then_inc(logits_made, 1)

            def expert_in(c, par):
                pe.wait_ge(h2T_ready, KD * (c + 1))
                for m in range(KI):
                    if not (first(c) and m < 2):
                        pe.wait_ge(hid_ready, KI * c + m - 1)
                    for z, col in ((a_ps, m * P), (b_ps, H + m * P)):
                        for k in range(KD):
                            last = nc.tensor.matmul(z[:, m % 2, :], w1s[:, k, col:col + P], h2T[:, par, k, :], start=(k == 0), stop=(k == KD - 1))
                    last.then_inc(z_made, 1)

            def expert_out(c):
                pe.wait_ge(hid_ready, KI * (c + 1))
                for h in range(2):
                    if not (first(c) and h == 0):
                        pe.wait_ge(y_used, 2 * c + h)
                    for i in range(2):
                        tt = 2 * h + i
                        for k in range(KI):
                            last = nc.tensor.matmul(y_ps[:, i, :], hid[:, k, tt * P:(tt + 1) * P], w2s[:, k, :], start=(k == 0), stop=(k == KI - 1))
                    last.then_inc(y_made, 1)

            def body(c, par, k, more):
                logits(c, par)
                expert_in(c, par)
                if more:
                    turn(c + 1, 1 - par)
                expert_out(c)

            turn(0, 0)
            pe.wait_ge(w_loaded, 4 * 16)
            bodies(pe, body)

        @block.scalar
        def _(act):
            def keep_turned(c, par):
                for k in range(KD):
                    act.wait_ge(turned, KD * c + k + 1)
                    if k == 0 and not first(c, 2):
                        act.wait_ge(z_made, KI * (c - 1))
                        act.wait_ge(logits_made, c - 1)
                    nc.scalar.activation(h2T[:, par, k, :], t_ps[:, k, :], ACT.Copy).then_inc(h2T_ready, 1)

            def body(c, par, k_, more):
                for m in range(KI):
                    act.wait_ge(z_made, KI * c + m + 1)
                    if not (first(c) and m < 2):
                        act.wait_ge(hid_ready, KI * c + m - 1)
                    nc.scalar.activation(sg[:, m % 2, :], b_ps[:, m % 2, :], ACT.Silu).then_inc(silu_ready, 1)
                if more:
                    keep_turned(c + 1, 1 - par)
                act.wait_ge(gate_step, 5 * c + 1)
                nc.scalar.activation(gs[:, 1, :], gs[:, 0, :], ACT.Exp).then_inc(gate_exp, 1)

            for e in range(NR):
                act.dma_start(t["w1r"][:, e], ins["w1"][e].rearrange("(k p) n -> p k n", p=P)).then_inc(w_routed, 16)
                act.dma_start(t["w2r"][:, e], ins["w2"][e].rearrange("(k p) n -> p k n", p=P)).then_inc(w_routed, 16)
            keep_turned(0, 0)
            bodies(act, body)
            act.wait_ge(w_routed, 2 * NR * 16)

        @block.vector
        def _(dve):
            def layernorm(c, par, k):
                dve.wait_ge(x1_loaded[par], 16 * k + 16)
                for tt in range(TT):
                    last = nc.vector.bn_stats(stats[:, tt, :], x1[:, par, tt, :])
                last.then_inc(ln_step, 1)
                hold(dve, ln_step, 2 * c + 1, held)
                for tt in range(TT):
                    last = nc.vector.bn_aggr(mv[:, tt, :], stats[:, tt, :])
                last.then_inc(ln_step, 1)
                dve.wait_ge(ln_step, 2 * c + 2)
                nc.vector.tensor_scalar(var[:], mv[:, :, 1], EPS, None, ALU.add).then_inc(var_ready, 1)

            def modulate(c, par, k):
                dve.wait_ge(rstd_ready, c + 1)
                if not first(c, 2):
                    dve.wait_ge(h2_stored[par], 16 * k)
                    dve.wait_ge(turned, KD * (c - 1))
                for tt in range(TT):
                    last = nc.vector.tensor_scalar(h2[:, par, tt, :], x1[:, par, tt, :], mv[:, tt, 0:1], rstd[:, tt:tt + 1], ALU.subtract, ALU.mult)
                last.then_inc(h2_step, 1)
                dve.wait_ge(h2_step, 2 * c + 1)
                nc.vector.tensor_tensor(h2[:, par], h2[:, par], mod2[:, 0, bass.ds(c // CPB, 1), :].to_broadcast([P, TT, D]), ALU.mult).then_inc(h2_step, 1)
                dve.wait_ge(h2_step, 2 * c + 2)
                nc.vector.tensor_tensor(h2[:, par], h2[:, par], mod2[:, 1, bass.ds(c // CPB, 1), :].to_broadcast([P, TT, D]), ALU.add).then_inc(h2_ready, 1)

            def gate_in(c):
                dve.wait_ge(logits_made, c + 1)
                nc.vector.tensor_copy(t["logits"][:, bass.ds(TT * c, TT), :], l_ps[:]).then_inc(logits_kept, 1)
                dve.wait_ge(logits_kept, c + 1)
                own = t["logits"][:, bass.ds(TT * c, TT), NR]
                nc.vector.tensor_tensor(gs[:, 0, :], own, own, ALU.subtract).then_inc(gate_step, 1)

            def gate_out(c):
                dve.wait_ge(gate_exp, c + 1)
                nc.vector.reciprocal(gs[:, 2, :], gs[:, 1, :]).then_inc(gate_step, 1)
                dve.wait_ge(gate_step, 5 * c + 2)
                nc.vector.tensor_tensor(gs[:, 3, :], gs[:, 1, :], gs[:, 2, :], ALU.mult).then_inc(gate_step, 1)
                dve.wait_ge(gate_step, 5 * c + 3)
                nc.vector.reciprocal(gs[:, 4, :], gs[:, 3, :]).then_inc(gate_step, 1)
                dve.wait_ge(gate_step, 5 * c + 4)
                nc.vector.tensor_tensor(gs[:, 5, :], gs[:, 3, :], gs[:, 4, :], ALU.mult).then_inc(gate_step, 1)

            def body(c, par, k, more):
                gate_in(c)
                for m in range(KI):
                    dve.wait_ge(silu_ready, KI * c + m + 1)
                    if m == 0 and not first(c):
                        dve.wait_ge(y_made, 2 * c)
                    nc.vector.tensor_tensor(hid[:, m, :], a_ps[:, m % 2, :], sg[:, m % 2, :], ALU.mult).then_inc(hid_ready, 1)
                    if m == 1 and more:
                        layernorm(c + 1, 1 - par, (c + 1) // 2)
                    if m == 2 and more:
                        modulate(c + 1, 1 - par, (c + 1) // 2)
                gate_out(c)
                dve.wait_ge(gate_step, 5 * c + 5)
                for tt in range(TT):
                    if tt % 2 == 0:
                        dve.wait_ge(y_made, 2 * c + tt // 2 + 1)
                    if tt == 0 and not first(c):
                        dve.wait_ge(acc_ready, c)
                    last = nc.vector.scalar_tensor_tensor(out=yg[:, tt, :], in0=y_ps[:, tt % 2, :], scalar=gs[:, 5, tt:tt + 1],
                                                          in1=mod2[:, 2, c // CPB, :], op0=ALU.mult, op1=ALU.mult)
                    if tt % 2 == 1:
                        last.then_inc(y_used, 1)
                dve.wait_ge(y_used, 2 * c + 2)
                nc.vector.tensor_tensor(x1[:, par], x1[:, par], yg[:], ALU.add).then_inc(acc_ready, 1)

            layernorm(0, 0, 0)
            dve.wait_ge(w_loaded, 4 * 16)
            modulate(0, 0, 0)
            bodies(dve, body)


def routing_program(nc, t, slots_dram):
    NE = NTILE * NR
    with ExitStack() as ctx:
        sem = lambda n: ctx.enter_context(nc.semaphore(n))
        sb = lambda n, s, dt=F32: ctx.enter_context(nc.sbuf_tensor(n, s, dt))
        logits, meta, owner = t["logits"], t["meta"], t["owner"]
        ex, p, mask, one, work = (sb(n, [P, NTILE, NR]) for n in ("ex", "prob", "mask", "one", "work"))
        mx, sm, rs, pm, taken, ss, pos = (sb(n, [P, NTILE]) for n in ("mx", "sm", "rs", "pm", "taken", "ss", "pos"))
        below, ones, each128, kidx = sb("below", [P, P]), sb("ones", [P, P]), sb("each128", [P, NTILE]), sb("kidx", [P, SLOT_TILES])
        incl, more = sb("incl", [P, NR, NTILE]), sb("more", [P, NR, NTILE])
        nt, tend, base, own = sb("nt", [P, NR]), sb("tend", [P, NR]), sb("base", [P, NR]), sb("own", [P, SLOT_TILES])
        posi, lane, slot = sb("posi", [P, NTILE], I32), sb("lane", [P, NTILE], I32), sb("slot", [P, NTILE], I32)
        info, slots = sb("info", [P, NTILE, 2], I32), sb("slots", [P, SLOT_TILES, 2], I32)
        prefix, total = (ctx.enter_context(nc.psum_tensor(n, [P, NTILE, NR], F32)) for n in ("prefix", "total"))
        consts, tri, step, exped, counted = sem("consts"), sem("tri"), sem("step"), sem("exped"), sem("counted")
        onehot, slots_ready, scattered, loaded = sem("onehot"), sem("slots_ready"), sem("scattered"), sem("loaded")
        shifted = sem("shifted")
        block = ctx.enter_context(nc.Block())

        @block.gpsimd
        def _(pool):
            nc.gpsimd.memset(below[:], 1.0).then_inc(tri, 1)
            nc.gpsimd.memset(ones[:], 1.0).then_inc(consts, 1)
            nc.gpsimd.iota(each128[:], pattern=[[P, NTILE]], base=0, channel_multiplier=0, allow_small_or_imprecise_dtypes=True).then_inc(consts, 1)
            nc.gpsimd.iota(kidx[:], pattern=[[1, SLOT_TILES]], base=0, channel_multiplier=0, allow_small_or_imprecise_dtypes=True).then_inc(consts, 1)
            nc.gpsimd.iota(info[:, :, 0], pattern=[[P, NTILE]], base=0, channel_multiplier=1).then_inc(consts, 1)
            pool.wait_ge(tri, 1)
            nc.gpsimd.affine_select(out=below[:], in_=below[:], compare_op=ALU.is_gt, fill=0.0, base=0,
                                    pattern=[[1, P]], channel_multiplier=-1).then_inc(consts, 1)
            pool.wait_ge(slots_ready, 1)
            pool.wait_ge(consts, 5)
            for j in range(NTILE):
                nc.gpsimd.indirect_dma_start(slots_dram, bass.IndirectOffsetOnAxis(slot[:, j:j + 1], 0), info[:, j, :], None).then_inc(scattered, 16)

        @block.sync
        def _(sp):
            sp.wait_ge(scattered, 16 * NTILE)
            sp.dma_start(slots[:], slots_dram.rearrange("(p k) w -> p k w", p=P)).then_inc(loaded, 16)
            sp.wait_ge(loaded, 16)

        @block.scalar
        def _(act):
            act.wait_ge(shifted, 1)
            nc.scalar.activation(ex[:], ex[:], ACT.Exp).then_inc(exped, 1)

        @block.tensor
        def _(pe):
            pe.wait_ge(onehot, 1)
            pe.wait_ge(consts, 5)
            flat = lambda x: x[:].rearrange("p j e -> p (j e)")
            nc.tensor.matmul(flat(prefix), below[:], flat(one), start=True, stop=True)
            nc.tensor.matmul(flat(total), ones[:], flat(one), start=True, stop=True).then_inc(counted, 1)

        @block.vector
        def _(dve):
            done = [0]

            def link(ins):
                done[0] += 1
                ins.then_inc(step, 1)
                dve.wait_ge(step, done[0])

            wide = lambda x: x[:].unsqueeze(2).to_broadcast([P, NTILE, NR])
            v = nc.vector
            routed = logits[:, :, 0:NR]
            link(v.tensor_reduce(mx[:], routed, AX_X, ALU.max))
            v.tensor_tensor(ex[:], routed, wide(mx), ALU.subtract).then_inc(shifted, 1)
            dve.wait_ge(exped, 1)
            link(v.tensor_reduce(sm[:], ex[:], AX_X, ALU.add))
            link(v.reciprocal(rs[:], sm[:]))
            link(v.tensor_tensor(p[:], ex[:], wide(rs), ALU.mult))
            link(v.tensor_reduce(pm[:], p[:], AX_X, ALU.max))
            link(v.tensor_tensor(mask[:], p[:], wide(pm), ALU.is_ge))
            link(v.tensor_copy(taken[:], mask[:, :, 0]))
            link(v.tensor_copy(one[:, :, 0], mask[:, :, 0]))
            for e in range(1, NR - 1):
                link(v.tensor_tensor(one[:, :, e], mask[:, :, e], taken[:], ALU.is_gt))
                link(v.tensor_tensor(taken[:], taken[:], mask[:, :, e], ALU.max))
            link(v.tensor_scalar(one[:, :, NR - 1], taken[:], -1.0, 1.0, ALU.mult, ALU.add))
            v.tensor_copy(work[:], one[:]).then_inc(onehot, 1)
            dve.wait_ge(onehot, 1)
            link(v.tensor_tensor(work[:], p[:], one[:], ALU.mult))
            link(v.tensor_reduce(ss[:], work[:], AX_X, ALU.add))
            link(v.reciprocal(rs[:], ss[:]))
            dve.wait_ge(consts, 5)
            link(v.tensor_tensor(info[:].bitcast(F32)[:, :, 1], ss[:], rs[:], ALU.mult))
            dve.wait_ge(counted, 1)
            for e in range(NR):
                link(v.tensor_tensor_scan(incl[:, e, :], ones[:, 0:NTILE], total[:, :, e], 0.0, ALU.mult, ALU.add))
            for e in range(NR):
                link(v.tensor_scalar(more[:, e, :], each128[:], incl[:, e, NTILE - 1:NTILE], None, ALU.is_lt))
            link(v.tensor_reduce(nt[:], more[:], AX_X, ALU.add))
            link(v.tensor_tensor_scan(tend[:], ones[:, 0:NR], nt[:], 0.0, ALU.mult, ALU.add))
            link(v.tensor_tensor(base[:], tend[:], nt[:], ALU.subtract))
            link(v.tensor_scalar(base[:], base[:], float(P), None, ALU.mult))
            link(v.tensor_tensor(work[:], prefix[:], incl[:].rearrange("p e j -> p j e"), ALU.add))
            link(v.tensor_tensor(work[:], work[:], total[:], ALU.subtract))
            link(v.tensor_tensor(work[:], work[:], base[:].unsqueeze(1).to_broadcast([P, NTILE, NR]), ALU.add))
            link(v.tensor_tensor(work[:], work[:], one[:], ALU.mult))
            link(v.tensor_reduce(pos[:], work[:], AX_X, ALU.add))
            link(v.tensor_copy(posi[:], pos[:]))
            link(v.tensor_scalar(lane[:], posi[:], P - 1, None, ALU.bitwise_and))
            link(v.tensor_scalar(posi[:], posi[:], P.bit_length() - 1, None, ALU.logical_shift_right))
            v.scalar_tensor_tensor(out=slot[:], in0=lane[:], scalar=float(SLOT_TILES), in1=posi[:], op0=ALU.mult, op1=ALU.add).then_inc(slots_ready, 1)
            link(v.tensor_scalar(own[:], kidx[:], tend[:, 0:1], None, ALU.is_ge))
            for e in range(1, NR):
                link(v.scalar_tensor_tensor(out=own[:], in0=kidx[:], scalar=tend[:, e:e + 1], in1=own[:], op0=ALU.is_ge, op1=ALU.add))
            link(v.tensor_scalar(owner[:], own[:], float(NR - 1), None, ALU.min))
            dve.wait_ge(loaded, 16)
            link(v.tensor_scalar(meta[:, :, 0], slots[:, :, 0], float(BATCH * SEQ - 1), None, ALU.min))
            link(v.tensor_scalar(meta[:, :, 1], meta[:, :, 0], SEQ.bit_length() - 1, None, ALU.logical_shift_right))
            link(v.tensor_copy(meta[:, :, 2:4], slots[:]))


def experts_program(nc, t, rows_dram, gb_dram, out):
    NB = 4
    with ExitStack() as ctx:
        sem = lambda n: ctx.enter_context(nc.semaphore(n))
        sb = lambda n, s, dt=F32: ctx.enter_context(nc.sbuf_tensor(n, s, dt))
        ps = lambda n, s: ctx.enter_context(nc.psum_tensor(n, s, F32))
        cur, rows, gbr = sb("cur", [P, NB, 4], I32), sb("rows_sb", [P, NB, 2 * D]), sb("gbr", [P, NB, D])
        outr = sb("outr", [P, NB, D])
        hT, sg, hid, hidT = sb("hT5", [P, 2, KD, P]), sb("sg5", [P, 2, H]), sb("hid5", [P, 2, H]), sb("hidT5", [P, KI, P])
        z = ps("z5", [P, 2, 2, H])
        t_ps, ht_ps, y_ps = ps("t5_ps", [P, KD, P]), ps("ht5_ps", [P, KI, P]), ps("y5_ps", [P, D])
        held = sem("held5")
        cur_ready, fetched = sem("cur_ready"), [sem(f"fetched{i}") for i in range(NB)]
        turned, hT_ready, z_made, silu_ready = sem("turned5"), sem("hT5_ready"), sem("z5_made"), sem("silu5_ready")
        hid_ready, hid_turned, hidT_ready, y_made = sem("hid5_ready"), sem("hid5_turned"), sem("hidT5_ready"), sem("y5_made")
        y_used, out_ready, stored = sem("y5_used"), sem("out5_ready"), [sem(f"stored{i}") for i in range(NB)]
        block = ctx.enter_context(nc.Block())
        N = SLOT_TILES
        first = lambda k, n: isinstance(k, int) and k < n

        def tile_at(k, d):
            if isinstance(k, int):
                return k + d, (k + d) % NB, (k + d) // NB
            return k + d, (1 + d) % NB, (k - 1) // NB + (1 + d) // NB

        def bodies(eng, body, straight=1):
            body(lambda d: tile_at(0, d))
            with eng.Fori(1, N - straight - NB + 1, NB) as k:
                for i in range(NB):
                    body(lambda d: tile_at(k, i + d))
            for k in range(N - straight, N):
                body(lambda d: tile_at(k, d))

        assert (N - 2) % NB == 0
        is_last = lambda k, n: isinstance(k, int) and k >= N - n

        @block.gpsimd
        def _(pool):
            def fetch(k, q, n):
                if not first(k, NB):
                    pool.wait_ge(stored[q], 16 * n)
                nc.gpsimd.tensor_copy(cur[:, q, :], t["meta"][:, k, :]).then_inc(cur_ready, 1)
                hold(pool, cur_ready, k + 1, held)
                nc.gpsimd.indirect_dma_start(rows[:, q, :], None, rows_dram, bass.IndirectOffsetOnAxis(cur[:, q, 0:1], 0)).then_inc(fetched[q], 16)
                nc.gpsimd.indirect_dma_start(gbr[:, q, :], None, gb_dram, bass.IndirectOffsetOnAxis(cur[:, q, 1:2], 0)).then_inc(fetched[q], 16)

            def store(k, q, n):
                hold(pool, out_ready, k + 1, held)
                nc.gpsimd.indirect_dma_start(out, bass.IndirectOffsetOnAxis(cur[:, q, 2:3], 0), outr[:, q, :], None,
                                             bounds_check=BATCH * SEQ - 1, oob_is_err=False).then_inc(stored[q], 16)

            def body(at):
                if not first(at(0)[0], 1):
                    store(*at(-1))
                if not is_last(at(0)[0], 2):
                    fetch(*at(2))

            for k in range(2):
                fetch(*tile_at(k, 0))
            bodies(pool, body, straight=1 + NB)
            store(*tile_at(N - 1, 0))
            for q in range(NB):
                pool.wait_ge(stored[q], 16 * ((N - 1 - q) // NB + 1))

        @block.tensor
        def _(pe):
            def turn(k, q, n):
                pe.wait_ge(fetched[q], 32 * n + 32)
                if not first(k, 1):
                    pe.wait_ge(hT_ready, k)
                for i in range(KD):
                    last = nc.tensor.transpose(t_ps[:, i, :], rows[:, q, i * P:(i + 1) * P], t["ident"][:])
                last.then_inc(turned, 1)

            def expert_in(k, q):
                e = pe.value_load(t["owner"][0:1, bass.ds(k, 1)], min_val=0, max_val=NR - 1)
                pe.wait_ge(hT_ready, k + 1)
                if not first(k, 2):
                    pe.wait_ge(hid_ready, k - 1)
                for half in range(2):
                    for i in range(KD):
                        last = nc.tensor.matmul(z[:, q % 2, half, :], hT[:, q % 2, i, :], t["w1r"][:, e, i, half * H:(half + 1) * H],
                                                start=(i == 0), stop=(i == KD - 1))
                last.then_inc(z_made, 1)

            def turn_hid(k, q):
                pe.wait_ge(hid_ready, k + 1)
                if not first(k, 1):
                    pe.wait_ge(hidT_ready, k)
                for i in range(KI):
                    last = nc.tensor.transpose(ht_ps[:, i, :], hid[:, q % 2, i * P:(i + 1) * P], t["ident"][:])
                last.then_inc(hid_turned, 1)

            def expert_out(k, q):
                e = pe.value_load(t["owner"][0:1, bass.ds(k, 1)], min_val=0, max_val=NR - 1)
                pe.wait_ge(hidT_ready, k + 1)
                if not first(k, 1):
                    pe.wait_ge(y_used, k)
                for i in range(KI):
                    last = nc.tensor.matmul(y_ps[:, :], hidT[:, i, :], t["w2r"][:, e, i, :], start=(i == 0), stop=(i == KI - 1))
                last.then_inc(y_made, 1)

            def body(at):
                k, q, n = at(0)
                expert_in(k, q)
                if not first(k, 1):
                    turn_hid(*at(-1)[:2])
                if not is_last(k, 1):
                    turn(*at(1))
                if not first(k, 1):
                    expert_out(*at(-1)[:2])

            turn(0, 0, 0)
            bodies(pe, body)
            turn_hid(N - 1, (N - 1) % NB)
            expert_out(N - 1, (N - 1) % NB)

        @block.scalar
        def _(act):
            def keep_turned(k, q):
                act.wait_ge(turned, k + 1)
                if not first(k, 2):
                    act.wait_ge(z_made, k - 1)
                nc.scalar.activation(hT[:, q % 2], t_ps[:], ACT.Copy).then_inc(hT_ready, 1)

            def keep_hid(k):
                act.wait_ge(hid_turned, k + 1)
                if not first(k, 1):
                    act.wait_ge(y_made, k)
                nc.scalar.activation(hidT[:], ht_ps[:], ACT.Copy).then_inc(hidT_ready, 1)

            def body(at):
                k, q, n = at(0)
                if not first(k, 1):
                    keep_hid(k - 1)
                if not is_last(k, 1):
                    keep_turned(k + 1, (q + 1) % NB)
                act.wait_ge(z_made, k + 1)
                if not first(k, 2):
                    act.wait_ge(hid_ready, k - 1)
                nc.scalar.activation(sg[:, q % 2, :], z[:, q % 2, 1, :], ACT.Silu).then_inc(silu_ready, 1)

            keep_turned(0, 0)
            bodies(act, body)
            keep_hid(N - 1)

        @block.vector
        def _(dve):
            def combine(k, q, n):
                dve.wait_ge(y_made, k + 1)
                dve.wait_ge(fetched[q], 32 * n + 32)
                if not first(k, NB):
                    dve.wait_ge(stored[q], 16 * n)
                nc.vector.scalar_tensor_tensor(out=outr[:, q, :], in0=y_ps[:, :], scalar=cur[:, q, 3:4].bitcast(F32), in1=gbr[:, q, :],
                                               op0=ALU.mult, op1=ALU.mult).then_inc(y_used, 1)
                dve.wait_ge(y_used, k + 1)
                nc.vector.tensor_tensor(outr[:, q, :], outr[:, q, :], rows[:, q, D:2 * D], ALU.add).then_inc(out_ready, 1)

            def body(at):
                k, q, n = at(0)
                dve.wait_ge(silu_ready, k + 1)
                if not first(k, 2):
                    dve.wait_ge(hid_turned, k - 1)
                nc.vector.tensor_tensor(hid[:, q % 2, :], z[:, q % 2, 0, :], sg[:, q % 2, :], ALU.mult).then_inc(hid_ready, 1)
                if not first(k, 1):
                    combine(*at(-1))

            bodies(dve, body)
            combine(*tile_at(N - 1, 0))


def build(nc, ins, out):
    dram = lambda n, s: nc.dram_tensor(n, s, F32, kind="Internal").ap()
    mod2_dram = dram("mod2_rows", [P, 3, BATCH, D])
    gb_dram, rows_dram = dram("gb_rows", [BATCH, D]), dram("token_rows", [BATCH * SEQ, 2 * D])
    slots_dram = nc.dram_tensor("slots_list", [P * SLOT_TILES, 2], I32, kind="Internal").ap()
    bc_dram, x1_dram = dram("bc_rows", [2 * STATE, T]), dram("x1", [BATCH * SEQ, D])
    with ExitStack() as ctx:
        sb = lambda n, s: ctx.enter_context(nc.sbuf_tensor(n, s, F32))
        keep = {"ident": sb("ident", [P, P]), "mhalf": sb("mhalf", [P, 8])}
        with ExitStack() as inner:
            sb = lambda n, s: inner.enter_context(nc.sbuf_tensor(n, s, F32))
            t = keep | {
                "spread": sb("spread", [P, SPC, P]), "gather": sb("gather", [P, DS]), "limits": sb("limits", [P, NCHUNK + 1, 2]), "state": sb("state", [P, NSET * NG]), "xpad": sb("xpad", [P, KI, T + KCONV - 1]),
                "a": sb("a", [P, NSET * NG]), "cw": sb("cw", [P, KI, KCONV]), "cb": sb("cb", [P, KI]), "dtb": sb("dtb", [P, KI]),
                "w_in": sb("w_in", [P, KD, 2 * DI]), "w_x": sb("w_x", [P, KI, PROJ]), "w_dt": sb("w_dt", [DT_RANK, DI]),
                "w_out": sb("w_out", [P, KI, D]), "w_conv": sb("w_conv", [P, KI, KCONV, P]), "sa": sb("sa", [P, KD, BATCH]),
                "ca": sb("ca", [P, KD, BATCH]), "ga": sb("ga", [P, BATCH, D])}
            setup_program(nc, ins, t, mod2_dram, gb_dram)
            mamba_program(nc, ins, t, bc_dram, x1_dram)
        with ExitStack() as inner:
            sb = lambda n, s, dt=F32: inner.enter_context(nc.sbuf_tensor(n, s, dt))
            t = keep | {"w1r": sb("w1r", [P, NR, KD, 2 * H]), "w2r": sb("w2r", [P, NR, KI, D]), "logits": sb("logits", [P, NTILE, NEXP]),
                        "meta": sb("meta", [P, SLOT_TILES, 4], I32), "owner": sb("owner", [P, SLOT_TILES], I32)}
            shared_program(nc, ins, t, mod2_dram, x1_dram, rows_dram, slots_dram)
            routing_program(nc, t, slots_dram)
            experts_program(nc, t, rows_dram, gb_dram, out)



def laid_out(x):
    import numpy as np
    a = {k: np.asarray(v) for k, v in x.items()}
    c = np.ascontiguousarray
    return {
        "x": c(a["L0_attn_x"].reshape(BATCH * SEQ, D)),
        "w_in": c(a["L0_attn_in_proj_w"].T), "conv_w": c(a["L0_attn_conv_w"].reshape(KI, P, KCONV).transpose(1, 0, 2)),
        "conv_b": c(a["L0_attn_conv_b"].reshape(KI, P).T),
        "w_x": c(a["L0_attn_x_proj_w"].T), "w_dt": c(a["L0_attn_dt_proj_w"].T), "dt_b": c(a["L0_attn_dt_proj_b"].reshape(KI, P).T),
        "a_cols": c(a["L0_attn_A_log"].reshape(NSET, DS, NF, NG).transpose(2, 1, 0, 3).reshape(P, NSET * NG)),
        "w_out": c(a["L0_attn_out_proj_w"].T), "wg": c(a["L0_ffn_Wg_DN"]), "w1": c(a["L0_ffn_Wl1_ND2H"]), "w2": c(a["L0_ffn_Wl2_NHD"]),
        "c": c(a["L0_c"].reshape(BATCH, KD, P).transpose(2, 1, 0)), "wmod": c(a["L0_wmod"]),
    }


def kernel(**inputs):
    import concourse.bacc as bacc
    from concourse.bass_utils import run_bass_kernel_spmd

    arrays = {f"in_{k}": v for k, v in laid_out(inputs).items()}
    nc = bacc.Bacc("TRN2", target_bir_lowering=False, num_devices=1)
    ins = {k[3:]: nc.dram_tensor(k, v.shape, mybir.dt.from_np(v.dtype), kind="ExternalInput").ap() for k, v in arrays.items()}
    out = nc.dram_tensor("out", [BATCH * SEQ, D], F32, kind="ExternalOutput").ap()
    build(nc, ins, out)
    r = run_bass_kernel_spmd(nc, [arrays], core_ids=[0])
    return r.results[0]["out"].reshape(BATCH, SEQ, D)
```

```python
from contextlib import ExitStack

import concourse.bass as bass
from concourse import mybir

F32 = mybir.dt.float32
I32 = mybir.dt.int32
ALU = mybir.AluOpType
ACT = mybir.ActivationFunctionType
AX_X = mybir.AxisListType.X

P = 128
BATCH, SEQ, D = 4, 2048, 256
DI, DT_RANK, STATE, KCONV = 512, 64, 16, 4
NEXP, H = 8, 512
NR = NEXP - 1
T = 512
NCHUNK = BATCH * SEQ // T
CPB = SEQ // T
TT = T // P
KD = D // P
KI = DI // P
DS = 32
NSET = DI // DS
NF = P // DS
NG = STATE // NF
SPC = P // DS
RING = 8
ABANK = 4
NBANK = 3
EPS = 1e-5
BIG = 3.4028234e38
NTILE = BATCH * SEQ // P
SLOT_TILES = NTILE + NR - 1
PROJ = DT_RANK + 2 * STATE
EMPTY = 1 << 20


def hold(eng, sem, value, held):
    eng.wait_ge(sem, value)
    eng.sem_inc(held, 1)


def setup_program(nc, ins, t, mod2_dram, gb_dram):
    with ExitStack() as ctx:
        sem = lambda n: ctx.enter_context(nc.semaphore(n))
        cT = ctx.enter_context(nc.sbuf_tensor("cT", [P, KD, BATCH], F32))
        cs = ctx.enter_context(nc.sbuf_tensor("cs", [P, KD, BATCH], F32))
        csb = ctx.enter_context(nc.sbuf_tensor("csb", [P, BATCH, KD, P], F32))
        wmod = ctx.enter_context(nc.sbuf_tensor("wmod", [P, KD, 6 * D], F32))
        rows = ctx.enter_context(nc.sbuf_tensor("rows", [P, 4, D], F32))
        mod2 = ctx.enter_context(nc.sbuf_tensor("mod2", [P, 3, BATCH, D], F32))
        pos = ctx.enter_context(nc.sbuf_tensor("posm", [P, 2, D], F32))
        pc = ctx.enter_context(nc.psum_tensor("pc", [P, 2 * KD, BATCH], F32))
        pr = ctx.enter_context(nc.psum_tensor("pr", [P, 2, 2, D], F32))
        c_loaded, zeroed, selectors = sem("c_loaded"), sem("zeroed"), sem("selectors")
        w_loaded, c_silu, c_spread = sem("w_loaded"), sem("c_silu"), sem("c_spread")
        cols_ready, cols_kept, row_ready, row_kept = sem("cols_ready"), sem("cols_kept"), sem("row_ready"), sem("row_kept")
        rows_step, a_loaded, a_exp, mod2_stored = sem("rows_step"), sem("a_loaded"), sem("a_exp"), sem("mod2_stored")
        block = ctx.enter_context(nc.Block())

        @block.sync
        def _(sp):
            sp.dma_start(cT[:], ins["c"]).then_inc(c_loaded, 16)
            sp.dma_start(wmod[:], ins["wmod"].rearrange("(k p) n -> p k n", p=P)).then_inc(c_loaded, 16)
            sp.dma_start(t["a"][:], ins["a_cols"]).then_inc(a_loaded, 16)
            sp.dma_start(t["cw"][:], ins["conv_w"]).then_inc(w_loaded, 16)
            sp.dma_start(t["cb"][:], ins["conv_b"]).then_inc(w_loaded, 16)
            sp.dma_start(t["dtb"][:], ins["dt_b"]).then_inc(w_loaded, 16)
            sp.dma_start(t["w_in"][:], ins["w_in"].rearrange("(k p) n -> p k n", p=P)).then_inc(w_loaded, 16)
            sp.dma_start(t["w_x"][:], ins["w_x"].rearrange("(k p) n -> p k n", p=P)).then_inc(w_loaded, 16)
            sp.dma_start(t["w_dt"][:], ins["w_dt"]).then_inc(w_loaded, 16)
            sp.dma_start(t["w_out"][:], ins["w_out"].rearrange("(k p) n -> p k n", p=P)).then_inc(w_loaded, 16)
            sp.wait_ge(w_loaded, 7 * 16)
            sp.wait_ge(rows_step, 5 * BATCH)
            sp.dma_start(mod2_dram, mod2[:]).then_inc(mod2_stored, 16)
            sp.dma_start(gb_dram.rearrange("(o b) d -> o b d", o=1), mod2[0:1, 2]).then_inc(mod2_stored, 16)
            sp.wait_ge(mod2_stored, 32)

        @block.gpsimd
        def _(pool):
            nc.gpsimd.memset(t["ident"][:], 0.0).then_inc(zeroed, 1)
            nc.gpsimd.memset(t["gather"][:], 0.0).then_inc(zeroed, 1)
            nc.gpsimd.memset(t["limits"][:, :, 0], BIG).then_inc(zeroed, 1)
            nc.gpsimd.memset(t["limits"][:, :, 1], -BIG).then_inc(zeroed, 1)
            nc.gpsimd.memset(t["mhalf"][:], -0.5).then_inc(zeroed, 1)
            nc.gpsimd.memset(t["state"][:], 0.0).then_inc(zeroed, 1)
            nc.gpsimd.memset(t["xpad"][:, :, 0:KCONV - 1], 0.0).then_inc(zeroed, 1)
            pool.wait_ge(zeroed, 7)
            nc.gpsimd.affine_select(out=t["ident"][:], in_=t["ident"][:], compare_op=ALU.not_equal, fill=1.0,
                                    base=0, pattern=[[-1, P]], channel_multiplier=1).then_inc(selectors, 1)
            nc.gpsimd.memset(t["limits"][:, 0:NCHUNK + 1:CPB, :], 0.0).then_inc(selectors, 1)
            for a in range(NF):
                nc.gpsimd.affine_select(out=t["gather"][:], in_=t["gather"][:], compare_op=ALU.not_equal, fill=1.0,
                                        base=-DS * a, pattern=[[-1, DS]], channel_multiplier=1).then_inc(selectors, 1)
                pool.wait_ge(selectors, 3 + a)

        @block.scalar
        def _(act):
            act.wait_ge(c_loaded, 2 * 16)
            nc.scalar.activation(cs[:], cT[:], ACT.Silu).then_inc(c_silu, 1)
            act.wait_ge(a_loaded, 16)
            nc.scalar.activation(t["a"][:], t["a"][:], ACT.Exp).then_inc(a_exp, 1)

        @block.vector
        def _(dve):
            dve.wait_ge(c_silu, 1)
            for b in range(BATCH):
                for kc in range(KD):
                    last = nc.vector.tensor_copy(csb[:, b, kc, :], cs[:, kc, b:b + 1].to_broadcast([P, P]))
            last.then_inc(c_spread, 1)
            dve.wait_ge(a_exp, 1)
            nc.vector.tensor_scalar(t["a"][:], t["a"][:], -1.0, None, ALU.mult)
            dve.wait_ge(selectors, 1)
            dve.wait_ge(w_loaded, 7 * 16)
            for j in range(KI):
                for k in range(KCONV):
                    nc.vector.tensor_scalar(t["w_conv"][:, j, k, :], t["ident"][:], t["cw"][:, j, k:k + 1], None, ALU.mult)
            dve.wait_ge(cols_ready, 1)
            nc.vector.tensor_copy(t["sa"][:], pc[:, 0:KD, :])
            nc.vector.tensor_scalar(t["ca"][:], pc[:, KD:2 * KD, :], 1.0, None, ALU.add).then_inc(cols_kept, 1)
            step = 0
            for b in range(BATCH):
                dve.wait_ge(row_ready, b + 1)
                nc.vector.tensor_copy(rows[:, 0:2, :], pr[:, 0, :, :]).then_inc(rows_step, 1)
                nc.vector.tensor_copy(mod2[:, 1, b, :], pr[:, 1, 0, :])
                nc.vector.tensor_scalar(mod2[:, 0, b, :], pr[:, 1, 1, :], 1.0, None, ALU.add).then_inc(row_kept, 1)
                dve.wait_ge(rows_step, step + 1)
                nc.vector.tensor_scalar(pos[:], rows[:, 0:2, :], 0.0, None, ALU.is_ge)
                nc.vector.tensor_scalar(rows[:, 2:4, :], rows[:, 0:2, :], -1.0, None, ALU.mult).then_inc(rows_step, 1)
                dve.wait_ge(rows_step, step + 2)
                nc.vector.tensor_tensor(rows[:, 2:4, :], rows[:, 2:4, :], rows[:, 0:2, :], ALU.max)
                nc.vector.tensor_scalar(pos[:], pos[:], 2.0, -1.0, ALU.mult, ALU.add).then_inc(rows_step, 1)
                dve.wait_ge(rows_step, step + 3)
                nc.vector.tensor_scalar(rows[:, 2:4, :], rows[:, 2:4, :], 0.25, None, ALU.max).then_inc(rows_step, 1)
                dve.wait_ge(rows_step, step + 4)
                nc.vector.tensor_tensor(t["ga"][:, b, :], rows[:, 2, :], pos[:, 0, :], ALU.mult)
                nc.vector.tensor_tensor(mod2[:, 2, b, :], rows[:, 3, :], pos[:, 1, :], ALU.mult).then_inc(rows_step, 1)
                step += 5
                dve.wait_ge(rows_step, step)

        @block.tensor
        def _(pe):
            pe.wait_ge(c_loaded, 2 * 16)
            pe.wait_ge(c_silu, 1)
            for n in range(2 * KD):
                for kc in range(KD):
                    last = nc.tensor.matmul(pc[:, n, :], wmod[:, kc, n * P:(n + 1) * P], cs[:, kc, :],
                                            start=(kc == 0), stop=(kc == KD - 1))
            last.then_inc(cols_ready, 1)
            pe.wait_ge(c_spread, 1)
            for b in range(BATCH):
                if b:
                    pe.wait_ge(row_kept, b)
                for n, part in enumerate((2, 5, 3, 4)):
                    for kc in range(KD):
                        last = nc.tensor.matmul(pr[:, n // 2, n % 2, :], csb[:, b, kc, :], wmod[:, kc, part * D:(part + 1) * D],
                                                start=(kc == 0), stop=(kc == KD - 1))
                last.then_inc(row_ready, 1)


def mamba_program(nc, ins, t, bc_dram, x1_dram):
    x_in = ins["x"].rearrange("(c t p) d -> c p t d", t=TT, p=P)
    x1_out = x1_dram.rearrange("(c t p) d -> c p t d", t=TT, p=P)
    with ExitStack() as ctx:
        sem = lambda n: ctx.enter_context(nc.semaphore(n))
        sb = lambda n, s: ctx.enter_context(nc.sbuf_tensor(n, s, F32))
        ps = lambda n, s: ctx.enter_context(nc.psum_tensor(n, s, F32))
        xin = sb("xin", [P, TT, D])
        hT = xin[:].rearrange("p t d -> p (t d)").rearrange("p (k t) -> p k t", k=KD)
        stats, mv, var, rstd = sb("stats", [P, TT, 6]), sb("mv", [P, TT, 2]), sb("var", [P, TT]), sb("rstd", [P, TT])
        xpad, us = t["xpad"], sb("us", [P, KI, T])
        res = sb("res", [P, 2, KI, T])
        xdbl_gy = sb("xdbl_gy", [P, T])
        xdbl, gy = xdbl_gy[0:PROJ, :], xdbl_gy[:].rearrange("p (h d) -> p h d", h=2)
        delta, xres = sb("delta", [P, KI, T]), sb("xres", [P, TT, D])
        du = us
        d_rep, u_rep = sb("d_rep", [P, 2, KI, T]), sb("u_rep", [P, 2, KI, T])
        relu = u_rep[:, 0]
        b_rep, c_rep = sb("b_rep", [P, 2, NG * T]), sb("c_rep", [P, 2, NG * T])
        hs = sb("hs", [P, RING, NG, T])
        state, bound = t["state"], sb("bound", [P, 2])
        banks = [ps(f"bank{i}", [P, T]) for i in range(NBANK)]
        y_ps = ps("y_ps", [P, T])
        dA = ps("dA", [P, ABANK, T])

        x_loaded, var_ready, rstd_ready, xn_ready = sem("x_loaded"), sem("var_ready"), sem("rstd_ready"), sem("xn_ready")
        ln_step, hT_ready = sem("ln_step"), sem("hT_ready")
        turned, xs_made, res_made, conv_made = sem("turned"), sem("xs_made"), sem("res_made"), sem("conv_made")
        xdbl_made, dt_made, out_made = sem("xdbl_made"), sem("dt_made"), sem("out_made")
        halo_ready = sem("halo_ready")
        xs_ready, us_pre, us_ready, res_pre, res_ready = sem("xs_ready"), sem("us_pre"), sem("us_ready"), sem("res_pre"), sem("res_ready")
        xdbl_ready, bc_kept, bc_loaded = sem("xdbl_ready"), sem("bc_kept"), sem("bc_loaded")
        sp_step, relu_ready, log_ready, delta_ready, du_ready = sem("sp_step"), sem("relu_ready"), sem("log_ready"), sem("delta_ready"), sem("du_ready")
        drep_loaded, urep_loaded = [sem("drep_loaded0"), sem("drep_loaded1")], [sem("urep_loaded0"), sem("urep_loaded1")]
        da_ready = sem("da_ready")
        dbu_done, scan_done, state_saved, hc_ready = sem("dbu_done"), sem("scan_done"), sem("state_saved"), sem("hc_ready")
        y_ready, yg_ready, gy_ready = sem("y_ready"), sem("yg_ready"), sem("gy_ready")
        held, bound_set = sem("held"), sem("bound_set")
        xres_loaded, x1_ready, x1_stored = sem("xres_loaded"), sem("x1_ready"), sem("x1_stored")
        block = ctx.enter_context(nc.Block())

        front = ([("T", k) for k in range(KD)] + [("XS", j) for j in range(KI)] + [("RS", 0), ("RS", 1)]
                 + [("CV", j) for j in range(KI)] + [("XP", 0), ("RS", 2), ("RS", 3)] + [("DT", j) for j in range(KI)])
        back = [("OP", 0), ("OP", 1)]
        bank_of = {g: i % NBANK for i, g in enumerate(front)} | {g: i + 1 for i, g in enumerate(back)}
        plan = {2: [("T", 0), ("T", 1)], 3: [("XS", 0), ("XS", 1)], 4: [("XS", 2), ("OP", 0)], 5: [("XS", 3), ("OP", 1)],
                6: [("RS", 0)], 7: [("RS", 1)], 8: [("CV", 0)], 9: [("CV", 1), ("CV", 2)], 10: [("CV", 3)],
                12: [("XP", 0)] + [("DT", j) for j in range(KI)], 13: [("RS", 2)], 14: [("RS", 3)]}
        order = [g for s in range(NSET) for g in plan.get(s, [])]
        SUM_AT = 2
        SILU_AT, LOG_AT, DELTA_AT = 11, 13, 13
        made = {"T": turned, "XS": xs_made, "RS": res_made, "CV": conv_made, "XP": xdbl_made, "DT": dt_made, "OP": out_made}
        kept = {"T": hT_ready, "XS": xs_ready, "RS": res_pre, "CV": us_pre, "XP": xdbl_ready, "DT": relu_ready, "OP": gy_ready}
        many = {"T": KD, "XS": KI, "RS": KI, "CV": KI, "XP": 1, "DT": KI, "OP": 2}

        def chunk_of(g, c):
            return 0 if c is None else c + 1 if g in front else c - 1

        def count(g, c):
            return many[g[0]] * chunk_of(g, c) + g[1] + 1

        def take_bank(pe, g, c):
            same = lambda x: bank_of[x] == bank_of[g]
            is_there = lambda x, b: x in front if isinstance(b, int) and b == 0 else x in back if isinstance(b, int) and b >= NCHUNK - 1 else True
            if c is None:
                before = [(x, None) for x in front[:front.index(g)] if same(x)]
            else:
                ahead = back[:back.index(g)] if isinstance(c, int) and c == NCHUNK else order[:order.index(g)]
                before = [(x, c) for x in ahead if same(x) and is_there(x, c)]
                if not before:
                    earlier = c - 1 if not (isinstance(c, int) and c == 0) else None
                    seq = front if earlier is None else order
                    before = [(x, earlier) for x in seq if same(x) and (earlier is None or is_there(x, earlier))]
                    if not before:
                        before = [(x, c - 2) for x in order if same(x)]
            if before:
                x, b = before[-1]
                pe.wait_ge(kept[x[0]], count(x, b))
            return banks[bank_of[g]]

        def read_bank(eng, g, c):
            eng.wait_ge(made[g[0]], count(g, c))
            return banks[bank_of[g]]

        def bodies(eng, body):
            body(0, 0, False, True)
            with eng.Fori(1, NCHUNK - 2, 2) as c:
                body(c, 1, True, True)
                body(c + 1, 0, True, True)
            body(NCHUNK - 1, 1, True, False)

        @block.sync
        def _(sp):
            def load_x(f):
                sp.dma_start(xin[:], x_in[f]).then_inc(x_loaded, 16)

            def spread_bc(f, par):
                sp.wait_ge(xdbl_ready, f + 1)
                sp.dma_start(bc_dram, xdbl[DT_RANK:PROJ, :]).then_inc(bc_kept, 16)
                hold(sp, bc_kept, 16 * f + 16, held)
                if not isinstance(f, int) or f >= 2:
                    sp.wait_ge(dbu_done, NSET * (f - 1))
                    sp.wait_ge(hc_ready, NSET * (f - 1))
                for n, rep in enumerate((b_rep, c_rep)):
                    for nf in range(NF):
                        r = n * STATE + nf * NG
                        sp.dma_start(rep[DS * nf:DS * nf + DS, par, :],
                                     bc_dram[r:r + NG, :].rearrange("n t -> (n t)").partition_broadcast(DS)).then_inc(bc_loaded, 16)

            pair = lambda c, q: [(d_rep, delta, delta_ready, da_ready, drep_loaded),
                                 (u_rep, du, du_ready, dbu_done, urep_loaded)]

            def replicate(c, q):
                for rep, rows, ready, used, sems in pair(c, q):
                    hold(sp, ready, c + 1, held)
                    if not (isinstance(c, int) and c == 0 and q < 2):
                        hold(sp, used, (NG if used is da_ready else 1) * (NSET * c + KI * (q - 1)), held)
                    for nf in range(NF):
                        sp.dma_start(rep[DS * nf:DS * nf + DS, q % 2], rows[DS * q:DS * q + DS, :, :]).then_inc(sems[q % 2], 16)

            def body(c, par, back_, front_, first=False, load=True):
                replicate(c, 1)
                if back_:
                    if not first:
                        hold(sp, x1_stored, 16 * (c - 1), held)
                    sp.dma_start(xres[:], x_in[c - 1]).then_inc(xres_loaded, 16)
                replicate(c, 2)
                replicate(c, 3)
                if back_:
                    hold(sp, x1_ready, 2 * c, held)
                    sp.dma_start(x1_out[c - 1], xres[:]).then_inc(x1_stored, 16)
                if front_:
                    if load:
                        hold(sp, res_made, KI * (c + 2), held)
                        sp.dma_start(xin[:], x_in[c + 2]).then_inc(x_loaded, 16)
                    spread_bc(c + 1, 1 - par)
                    replicate(c + 1, 0)

            load_x(0)
            sp.wait_ge(res_made, KI)
            load_x(1)
            spread_bc(0, 0)
            replicate(0, 0)
            body(0, 0, False, True)
            body(1, 1, True, True, first=True)
            with sp.Fori(2, NCHUNK - 3, 2) as c:
                body(c, 0, True, True)
                body(c + 1, 1, True, True)
            body(NCHUNK - 2, 0, True, True, load=False)
            body(NCHUNK - 1, 1, True, False)
            sp.wait_ge(x1_stored, 16 * (NCHUNK - 1))
            sp.dma_start(xres[:], x_in[NCHUNK - 1]).then_inc(xres_loaded, 16)
            sp.wait_ge(x1_ready, 2 * NCHUNK)
            sp.dma_start(x1_out[NCHUNK - 1], xres[:]).then_inc(x1_stored, 16)
            sp.wait_ge(x1_stored, 16 * NCHUNK)

        @block.tensor
        def _(pe):
            def group(g, c, f, par=0):
                kind, j = g
                ps_ = take_bank(pe, g, c)
                if kind == "T":
                    if j == 0:
                        pe.wait_ge(xn_ready, f + 1)
                    for tt in range(TT):
                        last = nc.tensor.transpose(ps_[:, tt * P:(tt + 1) * P], xin[:, tt, j * P:(j + 1) * P], t["ident"][:])
                elif kind in ("XS", "RS"):
                    col = j * P + (DI if kind == "RS" else 0)
                    pe.wait_ge(hT_ready, KD * f + KD)
                    for k in range(KD):
                        last = nc.tensor.matmul(ps_[:, :], t["w_in"][:, k, col:col + P], hT[:, k, :], start=(k == 0), stop=(k == KD - 1))
                elif kind == "CV":
                    pe.wait_ge(xs_ready, KI * f + j + 1)
                    for k in range(KCONV):
                        last = nc.tensor.matmul(ps_[:, :], t["w_conv"][:, j, k, :], xpad[:, j, k:k + T], start=(k == 0), stop=(k == KCONV - 1))
                elif kind == "XP":
                    pe.wait_ge(us_ready, f + 1)
                    for k in range(KI):
                        last = nc.tensor.matmul(ps_[0:PROJ, :], t["w_x"][:, k, :], us[:, k, :], start=(k == 0), stop=(k == KI - 1))
                elif kind == "DT":
                    pe.wait_ge(xdbl_ready, f + 1)
                    last = nc.tensor.matmul(ps_[:, :], t["w_dt"][:, j * P:(j + 1) * P], xdbl[0:DT_RANK, :], start=True, stop=True)
                elif kind == "OP":
                    pe.wait_ge(yg_ready, KI * c)
                    for h in range(2):
                        for k in range(KI):
                            tt = 2 * j + h
                            last = nc.tensor.matmul(ps_[:, h * D:(h + 1) * D], res[:, 1 - par, k, tt * P:(tt + 1) * P], t["w_out"][:, k, :],
                                                    start=(k == 0), stop=(k == KI - 1))
                last.then_inc(made[kind], 1)

            def sum_states(c, j):
                pe.wait_ge(hc_ready, NSET * c + SPC * (j + 1))
                if not (isinstance(c, int) and c == 0 and j == 0):
                    pe.wait_ge(yg_ready, KI * c + j)
                for g in range(NG):
                    for q in range(SPC):
                        last = nc.tensor.matmul(y_ps[DS * q:DS * q + DS, :], t["gather"][:], hs[:, (SPC * j + q) % RING, g, :],
                                                start=(g == 0), stop=(g == NG - 1), skip_group_check=True,
                                                tile_position=(0, DS * q))
                last.then_inc(y_ready, 1)

            def body(c, par, back_, front_):
                for s in range(NSET):
                    for g in plan.get(s, []):
                        if front_ if g in front else back_:
                            group(g, c, c + 1, par)
                    if s == SUM_AT and back_:
                        sum_states(c - 1, KI - 1)
                    if s > SPC and s % SPC == SUM_AT:
                        sum_states(c, s // SPC - 1)

            for g in front:
                group(g, None, 0)
            bodies(pe, body)
            sum_states(NCHUNK - 1, KI - 1)
            for g in back:
                group(g, NCHUNK, None, 0)

        @block.scalar
        def _(act):
            def group(g, c, f, half, first=False):
                kind, j = g
                if kind == "OP":
                    return
                ps_ = read_bank(act, g, c)
                b = f // CPB
                if kind == "T":
                    if j == 0:
                        act.wait_ge(turned, KD * (f + 1))
                    nc.scalar.activation(hT[:, j, :], ps_[:, :], ACT.Identity, scale=t["ca"][:, j, bass.ds(b, 1)],
                                         bias=t["sa"][:, j, bass.ds(b, 1)]).then_inc(hT_ready, 1)
                elif kind == "XS":
                    if j == 0 and not first:
                        act.wait_ge(halo_ready, f)
                    nc.scalar.activation(xpad[:, j, KCONV - 1:], ps_[:, :], ACT.Copy).then_inc(xs_ready, 1)
                elif kind == "RS":
                    if j == 0 and not first and not (isinstance(f, int) and f == 1):
                        act.wait_ge(out_made, 2 * (f - 1))
                    nc.scalar.activation(res[:, half, j, :], ps_[:, :], ACT.Copy).then_inc(res_pre, 1)
                elif kind == "CV":
                    if j == 0 and not first:
                        for n in range(2):
                            act.wait_ge(urep_loaded[n], 16 * NF * 2 * f)
                    nc.scalar.activation(us[:, j, :], ps_[:, :], ACT.Identity, bias=t["cb"][:, j:j + 1]).then_inc(us_pre, 1)
                elif kind == "XP":
                    if not first:
                        act.wait_ge(dt_made, KI * f)
                        act.wait_ge(bc_kept, 16 * f)
                        if not (isinstance(f, int) and f == 1):
                            act.wait_ge(x1_ready, 2 * (f - 1))
                    nc.scalar.activation(xdbl[:, :], ps_[0:PROJ, :], ACT.Copy).then_inc(xdbl_ready, 1)
                elif kind == "DT":
                    n = KI * f + j
                    if j == 0 and not first:
                        for i in range(2):
                            act.wait_ge(drep_loaded[i], 16 * NF * 2 * f)
                        act.wait_ge(dbu_done, NSET * (f - 1) + NSET - KI)
                    nc.scalar.activation(delta[:, j, :], ps_[:, :], ACT.Abs, bias=t["dtb"][:, j:j + 1]).then_inc(sp_step, 1)
                    nc.scalar.activation(relu[:, j, :], ps_[:, :], ACT.Relu, bias=t["dtb"][:, j:j + 1]).then_inc(relu_ready, 1)
                    act.wait_ge(sp_step, 2 * n + 1)
                    nc.scalar.activation(delta[:, j, :], delta[:, j, :], ACT.Exp, scale=-1.0).then_inc(sp_step, 1)

            def logs(f):
                act.wait_ge(sp_step, 2 * KI * f + 2 * KI)
                nc.scalar.activation(delta[:], delta[:], ACT.Ln, bias=1.0).then_inc(log_ready, 1)

            def silu_u(f):
                act.wait_ge(us_pre, KI * f + KI)
                nc.scalar.activation(us[:], us[:], ACT.Silu).then_inc(us_ready, 1)

            def silu_res(f, half):
                act.wait_ge(res_pre, KI * f + KI)
                nc.scalar.activation(res[:, half], res[:, half], ACT.Silu).then_inc(res_ready, 1)

            def exps(c, s):
                q, j = divmod(s, KI)
                if j == 0:
                    act.wait_ge(drep_loaded[q % 2], 16 * NF * (2 * c + q // 2 + 1))
                for g in range(NG):
                    u = NG * s + g
                    if not (isinstance(c, int) and c == 0 and u < ABANK):
                        act.wait_ge(scan_done, NG * NSET * c + u - ABANK + 1)
                    nc.scalar.activation(dA[:, u % ABANK, :], d_rep[:, q % 2, j, :], ACT.Exp, scale=t["a"][:, u:u + 1]).then_inc(da_ready, 1)

            def body(c, par, back_, front_):
                for s in range(NSET):
                    exps(c, s)
                    if s == 0:
                        silu_res(c, par)
                    if front_:
                        for g in plan.get(s, []):
                            group(g, c, c + 1, 1 - par)
                        if s == SILU_AT:
                            silu_u(c + 1)
                        if s == LOG_AT:
                            logs(c + 1)

            for g in front:
                if g == ("XP", 0):
                    silu_u(0)
                group(g, None, 0, 0, first=True)
            logs(0)
            bodies(act, body)

        @block.vector
        def _(dve):
            def layernorm(f, first=False):
                dve.wait_ge(x_loaded, 16 * f + 16)
                for tt in range(TT):
                    last = nc.vector.bn_stats(stats[:, tt, :], xin[:, tt, :])
                last.then_inc(ln_step, 1)
                hold(dve, ln_step, 2 * f + 1, held)
                for tt in range(TT):
                    last = nc.vector.bn_aggr(mv[:, tt, :], stats[:, tt, :])
                last.then_inc(ln_step, 1)
                dve.wait_ge(ln_step, 2 * f + 2)
                nc.vector.tensor_scalar(var[:], mv[:, :, 1], EPS, None, ALU.add).then_inc(var_ready, 1)

            def normalize(f):
                dve.wait_ge(rstd_ready, f + 1)
                for tt in range(TT):
                    last = nc.vector.tensor_scalar(xin[:, tt, :], xin[:, tt, :], mv[:, tt, 0:1], rstd[:, tt:tt + 1], ALU.subtract, ALU.mult)
                last.then_inc(xn_ready, 1)

            def halo(f):
                dve.wait_ge(conv_made, KI * f)
                nc.vector.tensor_scalar(xpad[:, :, 0:KCONV - 1], xpad[:, :, T:T + KCONV - 1], t["limits"][:, bass.ds(f, 1), 0],
                                        t["limits"][:, bass.ds(f, 1), 1], ALU.min, ALU.max).then_inc(halo_ready, 1)

            def deltas(f):
                dve.wait_ge(relu_ready, KI * f + KI)
                dve.wait_ge(log_ready, f + 1)
                nc.vector.tensor_tensor(delta[:], delta[:], relu, ALU.add).then_inc(delta_ready, 1)
                dve.wait_ge(delta_ready, f + 1)
                dve.wait_ge(us_ready, f + 1)
                dve.wait_ge(xdbl_made, f + 1)
                nc.vector.tensor_tensor(us[:], delta[:], us[:], ALU.mult).then_inc(du_ready, 1)

            def states_in(c, s, par):
                n = NSET * c + s
                slot = s % RING
                q, j = divmod(s, KI)
                if j == 0:
                    dve.wait_ge(urep_loaded[q % 2], 16 * NF * (2 * c + q // 2 + 1))
                    if not (isinstance(c, int) and c == 0 and q < RING // KI):
                        dve.wait_ge(y_ready, SPC * c + q - RING // KI + 1)
                if s == 0:
                    dve.wait_ge(bc_loaded, 16 * 2 * NF * (c + 1))
                nc.vector.tensor_tensor(hs[:, slot], u_rep[:, q % 2, j, :].unsqueeze(1).to_broadcast([P, NG, T]),
                                        b_rep[:, par, :].rearrange("p (g t) -> p g t", g=NG), ALU.mult).then_inc(dbu_done, 1)

            def scan_set(c, s):
                n = NSET * c + s
                slot = s % RING
                dve.wait_ge(dbu_done, n + 1)
                if not (isinstance(c, int) and c == 0):
                    dve.wait_ge(state_saved, NSET * (c - 1) + s + 1)
                for g in range(NG):
                    u = NG * s + g
                    dve.wait_ge(da_ready, NG * n + g + 1)
                    nc.vector.tensor_tensor_scan(hs[:, slot, g, :], dA[:, u % ABANK, :], hs[:, slot, g, :], state[:, u:u + 1],
                                                 ALU.mult, ALU.add).then_inc(scan_done, 1)

            def gate_y(c, j, half):
                dve.wait_ge(y_ready, KI * c + j + 1)
                if j == 0:
                    dve.wait_ge(res_ready, c + 1)
                nc.vector.tensor_tensor(res[:, half, j, :], y_ps[:], res[:, half, j, :], ALU.mult).then_inc(yg_ready, 1)

            def residual(c, j):
                g = ("OP", j)
                ps_ = read_bank(dve, g, c)
                if j == 0:
                    dve.wait_ge(xres_loaded, 16 * c)
                if j:
                    dve.wait_ge(x1_ready, 2 * (c - 1) + j)
                nc.vector.tensor_tensor(gy, ps_[:].rearrange("p (h d) -> p h d", h=2),
                                        t["ga"][:, bass.ds((c - 1) // CPB, 1), :].to_broadcast([P, 2, D]), ALU.mult).then_inc(gy_ready, 1)
                dve.wait_ge(gy_ready, 2 * (c - 1) + j + 1)
                nc.vector.tensor_tensor(xres[:, 2 * j:2 * j + 2, :], xres[:, 2 * j:2 * j + 2, :], gy, ALU.add).then_inc(x1_ready, 1)

            def body(c, par, back_, front_):
                states_in(c, 0, par)
                for s in range(NSET):
                    if (s + 1) % KI:
                        states_in(c, s + 1, par)
                    scan_set(c, s)
                    if (s + 1) % KI == 0 and s + 1 < NSET:
                        states_in(c, s + 1, par)
                    if front_:
                        if s == 0:
                            layernorm(c + 1)
                            halo(c + 1)
                        if s == 1:
                            normalize(c + 1)
                    if back_ and s == 3:
                        gate_y(c - 1, SPC - 1, 1 - par)
                    if back_ and s in (6, 7):
                        residual(c, s - 6)
                    if s > SPC and s % SPC == 3:
                        gate_y(c, s // SPC - 1, par)
                    if front_ and s == DELTA_AT:
                        deltas(c + 1)

            layernorm(0)
            normalize(0)
            deltas(0)
            bodies(dve, body)
            gate_y(NCHUNK - 1, KI - 1, 1)
            residual(NCHUNK, 0)
            residual(NCHUNK, 1)

        @block.gpsimd
        def _(pool):
            def rsqrt(f):
                pool.wait_ge(var_ready, f + 1)
                nc.gpsimd.tensor_tensor(rstd[:], var[:], t["mhalf"][:, 0:TT], ALU.pow).then_inc(rstd_ready, 1)

            def body(c, par, back_, front_):
                if not (isinstance(c, int) and c == 0):
                    pool.wait_ge(state_saved, NSET * c)
                nc.gpsimd.tensor_copy(bound[:], t["limits"][:, c + 1, :]).then_inc(bound_set, 1)
                pool.wait_ge(bound_set, c + 1)
                for s in range(NSET):
                    n = NSET * c + s
                    slot = s % RING
                    hold(pool, scan_done, NG * (n + 1), held)
                    nc.gpsimd.tensor_scalar(state[:, NG * s:NG * s + NG], hs[:, slot, :, T - 1], bound[:, 0:1], bound[:, 1:2], ALU.min, ALU.max).then_inc(state_saved, 1)
                    if s == 0:
                        pool.wait_ge(bc_loaded, 16 * 2 * NF * (c + 1))
                    pool.wait_ge(state_saved, n + 1)
                    nc.gpsimd.tensor_tensor(hs[:, slot, :, :], hs[:, slot, :, :],
                                            c_rep[:, par, :].rearrange("p (g t) -> p g t", g=NG), ALU.mult).then_inc(hc_ready, 1)
                    if s == 0 and front_:
                        rsqrt(c + 1)

            rsqrt(0)
            bodies(pool, body)


def shared_program(nc, ins, t, mod2_dram, x1_dram, rows_dram, slots_dram):
    x1_in = x1_dram.rearrange("(c t p) d -> c p t d", t=TT, p=P)
    rows_out = rows_dram.rearrange("(c t p) (w d) -> w c p t d", t=TT, p=P, w=2)
    with ExitStack() as ctx:
        sem = lambda n: ctx.enter_context(nc.semaphore(n))
        sb = lambda n, s, dt=F32: ctx.enter_context(nc.sbuf_tensor(n, s, dt))
        ps = lambda n, s: ctx.enter_context(nc.psum_tensor(n, s, F32))
        mod2, wg = sb("mod2_sb", [P, 3, BATCH, D]), sb("wg_sb", [P, KD, NEXP])
        w1s, w2s = sb("w1s", [P, KD, 2 * H]), sb("w2s", [P, KI, D])
        x1, h2, h2T = sb("x1_sb", [P, 2, TT, D]), sb("h2", [P, 2, TT, D]), sb("h2T", [P, 2, KD, T])
        stats, mv, var, rstd = sb("stats2", [P, TT, 6]), sb("mv2", [P, TT, 2]), sb("var2", [P, TT]), sb("rstd2", [P, TT])
        gs = sb("gs", [P, 6, TT])
        sg, hid = sb("sg", [P, 2, T]), sb("hid", [P, KI, T])
        yg = sb("yg", [P, TT, D])
        empty = sb("empty", [P, SLOT_TILES, 2], I32)
        t_ps, a_ps, b_ps = ps("t_ps", [P, KD, T]), ps("a_ps", [P, 2, T]), ps("b_ps", [P, 2, T])
        y_ps, l_ps = ps("y2_ps", [P, 2, D]), ps("l_ps", [P, TT, NEXP])

        w_loaded, w_routed, x1_loaded = sem("w2_loaded"), sem("w_routed"), [sem("x1_loaded0"), sem("x1_loaded1")]
        held = sem("held3")
        empty_set, slots_set, ln_step, var_ready, rstd_ready = sem("empty_set"), sem("slots_set"), sem("ln2_step"), sem("var2_ready"), sem("rstd2_ready")
        h2_step, h2_ready, h2_stored = sem("h2_step"), sem("h2_ready"), [sem("h2_stored0"), sem("h2_stored1")]
        turned, h2T_ready, logits_made, logits_kept = sem("turned2"), sem("h2T_ready"), sem("logits_made"), sem("logits_kept")
        gate_step, gate_exp, gate_ready = sem("gate_step"), sem("gate_exp"), sem("gate_ready")
        z_made, silu_ready, hid_ready, y_made, y_used = sem("z_made"), sem("silu_ready"), sem("hid_ready"), sem("y_made"), sem("y_used")
        acc_ready, acc_stored = sem("acc_ready"), [sem("acc_stored0"), sem("acc_stored1")]
        block = ctx.enter_context(nc.Block())

        def bodies(eng, body):
            body(0, 0, 0, True)
            with eng.Fori(1, NCHUNK - 2, 2) as c:
                body(c, 1, (c - 1) // 2, True)
                body(c + 1, 0, (c + 1) // 2, True)
            body(NCHUNK - 1, 1, NCHUNK // 2 - 1, False)

        first = lambda c, n=1: isinstance(c, int) and c < n

        @block.sync
        def _(sp):
            def load(c, par):
                sp.dma_start(x1[:, par], x1_in[c]).then_inc(x1_loaded[par], 16)

            def body(c, par, k, more):
                if more:
                    if not first(c):
                        hold(sp, acc_stored[1 - par], 16 * ((c + 1) // 2), held)
                    load(c + 1, 1 - par)
                sp.wait_ge(h2_ready, c + 1)
                sp.dma_start(rows_out[0, c], h2[:, par]).then_inc(h2_stored[par], 16)
                sp.wait_ge(acc_ready, c + 1)
                sp.dma_start(rows_out[1, c], x1[:, par]).then_inc(acc_stored[par], 16)

            load(0, 0)
            sp.dma_start(mod2[:], mod2_dram).then_inc(w_loaded, 16)
            sp.dma_start(wg[:], ins["wg"].rearrange("(k p) n -> p k n", p=P)).then_inc(w_loaded, 16)
            sp.dma_start(w1s[:], ins["w1"][NEXP - 1].rearrange("(k p) n -> p k n", p=P)).then_inc(w_loaded, 16)
            sp.dma_start(w2s[:], ins["w2"][NEXP - 1].rearrange("(k p) n -> p k n", p=P)).then_inc(w_loaded, 16)
            bodies(sp, body)
            sp.wait_ge(empty_set, 2)
            sp.dma_start(slots_dram.rearrange("(p k) w -> p k w", p=P), empty[:]).then_inc(slots_set, 16)
            sp.wait_ge(slots_set, 16)
            for par in range(2):
                sp.wait_ge(h2_stored[par], 16 * NCHUNK // 2)
                sp.wait_ge(acc_stored[par], 16 * NCHUNK // 2)

        @block.gpsimd
        def _(pool):
            def rsqrt(c):
                pool.wait_ge(var_ready, c + 1)
                nc.gpsimd.tensor_tensor(rstd[:], var[:], t["mhalf"][:, 0:TT], ALU.pow).then_inc(rstd_ready, 1)

            nc.gpsimd.memset(empty[:, :, 0], EMPTY).then_inc(empty_set, 1)
            nc.gpsimd.memset(empty[:, :, 1], 0).then_inc(empty_set, 1)
            rsqrt(0)
            bodies(pool, lambda c, par, k, more: rsqrt(c + 1) if more else None)

        @block.tensor
        def _(pe):
            def turn(c, par):
                pe.wait_ge(h2_ready, c + 1)
                for k in range(KD):
                    if not first(c):
                        pe.wait_ge(h2T_ready, KD * (c - 1) + k + 1)
                    for tt in range(TT):
                        last = nc.tensor.transpose(t_ps[:, k, tt * P:(tt + 1) * P], h2[:, par, tt, k * P:(k + 1) * P], t["ident"][:])
                    last.then_inc(turned, 1)

            def logits(c, par):
                pe.wait_ge(h2T_ready, KD * (c + 1))
                if not first(c):
                    pe.wait_ge(logits_kept, c)
                for tt in range(TT):
                    for k in range(KD):
                        last = nc.tensor.matmul(l_ps[:, tt, :], h2T[:, par, k, tt * P:(tt + 1) * P], wg[:, k, :], start=(k == 0), stop=(k == KD - 1))
                last.then_inc(logits_made, 1)

            def expert_in(c, par):
                pe.wait_ge(h2T_ready, KD * (c + 1))
                for m in range(KI):
                    if not (first(c) and m < 2):
                        pe.wait_ge(hid_ready, KI * c + m - 1)
                    for z, col in ((a_ps, m * P), (b_ps, H + m * P)):
                        for k in range(KD):
                            last = nc.tensor.matmul(z[:, m % 2, :], w1s[:, k, col:col + P], h2T[:, par, k, :], start=(k == 0), stop=(k == KD - 1))
                    last.then_inc(z_made, 1)

            def expert_out(c):
                pe.wait_ge(hid_ready, KI * (c + 1))
                for h in range(2):
                    if not (first(c) and h == 0):
                        pe.wait_ge(y_used, 2 * c + h)
                    for i in range(2):
                        tt = 2 * h + i
                        for k in range(KI):
                            last = nc.tensor.matmul(y_ps[:, i, :], hid[:, k, tt * P:(tt + 1) * P], w2s[:, k, :], start=(k == 0), stop=(k == KI - 1))
                    last.then_inc(y_made, 1)

            def body(c, par, k, more):
                logits(c, par)
                expert_in(c, par)
                if more:
                    turn(c + 1, 1 - par)
                expert_out(c)

            turn(0, 0)
            pe.wait_ge(w_loaded, 4 * 16)
            bodies(pe, body)

        @block.scalar
        def _(act):
            def keep_turned(c, par):
                for k in range(KD):
                    act.wait_ge(turned, KD * c + k + 1)
                    if k == 0 and not first(c, 2):
                        act.wait_ge(z_made, KI * (c - 1))
                        act.wait_ge(logits_made, c - 1)
                    nc.scalar.activation(h2T[:, par, k, :], t_ps[:, k, :], ACT.Copy).then_inc(h2T_ready, 1)

            def body(c, par, k_, more):
                for m in range(KI):
                    act.wait_ge(z_made, KI * c + m + 1)
                    if not (first(c) and m < 2):
                        act.wait_ge(hid_ready, KI * c + m - 1)
                    nc.scalar.activation(sg[:, m % 2, :], b_ps[:, m % 2, :], ACT.Silu).then_inc(silu_ready, 1)
                if more:
                    keep_turned(c + 1, 1 - par)
                act.wait_ge(gate_step, 5 * c + 1)
                nc.scalar.activation(gs[:, 1, :], gs[:, 0, :], ACT.Exp).then_inc(gate_exp, 1)

            for e in range(NR):
                act.dma_start(t["w1r"][:, e], ins["w1"][e].rearrange("(k p) n -> p k n", p=P)).then_inc(w_routed, 16)
                act.dma_start(t["w2r"][:, e], ins["w2"][e].rearrange("(k p) n -> p k n", p=P)).then_inc(w_routed, 16)
            keep_turned(0, 0)
            bodies(act, body)
            act.wait_ge(w_routed, 2 * NR * 16)

        @block.vector
        def _(dve):
            def layernorm(c, par, k):
                dve.wait_ge(x1_loaded[par], 16 * k + 16)
                for tt in range(TT):
                    last = nc.vector.bn_stats(stats[:, tt, :], x1[:, par, tt, :])
                last.then_inc(ln_step, 1)
                hold(dve, ln_step, 2 * c + 1, held)
                for tt in range(TT):
                    last = nc.vector.bn_aggr(mv[:, tt, :], stats[:, tt, :])
                last.then_inc(ln_step, 1)
                dve.wait_ge(ln_step, 2 * c + 2)
                nc.vector.tensor_scalar(var[:], mv[:, :, 1], EPS, None, ALU.add).then_inc(var_ready, 1)

            def modulate(c, par, k):
                dve.wait_ge(rstd_ready, c + 1)
                if not first(c, 2):
                    dve.wait_ge(h2_stored[par], 16 * k)
                    dve.wait_ge(turned, KD * (c - 1))
                for tt in range(TT):
                    last = nc.vector.tensor_scalar(h2[:, par, tt, :], x1[:, par, tt, :], mv[:, tt, 0:1], rstd[:, tt:tt + 1], ALU.subtract, ALU.mult)
                last.then_inc(h2_step, 1)
                dve.wait_ge(h2_step, 2 * c + 1)
                nc.vector.tensor_tensor(h2[:, par], h2[:, par], mod2[:, 0, bass.ds(c // CPB, 1), :].to_broadcast([P, TT, D]), ALU.mult).then_inc(h2_step, 1)
                dve.wait_ge(h2_step, 2 * c + 2)
                nc.vector.tensor_tensor(h2[:, par], h2[:, par], mod2[:, 1, bass.ds(c // CPB, 1), :].to_broadcast([P, TT, D]), ALU.add).then_inc(h2_ready, 1)

            def gate_in(c):
                dve.wait_ge(logits_made, c + 1)
                nc.vector.tensor_copy(t["logits"][:, bass.ds(TT * c, TT), :], l_ps[:]).then_inc(logits_kept, 1)
                dve.wait_ge(logits_kept, c + 1)
                own = t["logits"][:, bass.ds(TT * c, TT), NR]
                nc.vector.tensor_tensor(gs[:, 0, :], own, own, ALU.subtract).then_inc(gate_step, 1)

            def gate_out(c):
                dve.wait_ge(gate_exp, c + 1)
                nc.vector.reciprocal(gs[:, 2, :], gs[:, 1, :]).then_inc(gate_step, 1)
                dve.wait_ge(gate_step, 5 * c + 2)
                nc.vector.tensor_tensor(gs[:, 3, :], gs[:, 1, :], gs[:, 2, :], ALU.mult).then_inc(gate_step, 1)
                dve.wait_ge(gate_step, 5 * c + 3)
                nc.vector.reciprocal(gs[:, 4, :], gs[:, 3, :]).then_inc(gate_step, 1)
                dve.wait_ge(gate_step, 5 * c + 4)
                nc.vector.tensor_tensor(gs[:, 5, :], gs[:, 3, :], gs[:, 4, :], ALU.mult).then_inc(gate_step, 1)

            def body(c, par, k, more):
                gate_in(c)
                for m in range(KI):
                    dve.wait_ge(silu_ready, KI * c + m + 1)
                    if m == 0 and not first(c):
                        dve.wait_ge(y_made, 2 * c)
                    nc.vector.tensor_tensor(hid[:, m, :], a_ps[:, m % 2, :], sg[:, m % 2, :], ALU.mult).then_inc(hid_ready, 1)
                    if m == 0 and more:
                        layernorm(c + 1, 1 - par, (c + 1) // 2)
                    if m == 1 and more:
                        modulate(c + 1, 1 - par, (c + 1) // 2)
                gate_out(c)
                dve.wait_ge(gate_step, 5 * c + 5)
                for tt in range(TT):
                    if tt % 2 == 0:
                        dve.wait_ge(y_made, 2 * c + tt // 2 + 1)
                    if tt == 0 and not first(c):
                        dve.wait_ge(acc_ready, c)
                    last = nc.vector.scalar_tensor_tensor(out=yg[:, tt, :], in0=y_ps[:, tt % 2, :], scalar=gs[:, 5, tt:tt + 1],
                                                          in1=mod2[:, 2, c // CPB, :], op0=ALU.mult, op1=ALU.mult)
                    if tt % 2 == 1:
                        last.then_inc(y_used, 1)
                dve.wait_ge(y_used, 2 * c + 2)
                nc.vector.tensor_tensor(x1[:, par], x1[:, par], yg[:], ALU.add).then_inc(acc_ready, 1)

            layernorm(0, 0, 0)
            dve.wait_ge(w_loaded, 4 * 16)
            modulate(0, 0, 0)
            bodies(dve, body)


def routing_program(nc, t, slots_dram):
    NE = NTILE * NR
    with ExitStack() as ctx:
        sem = lambda n: ctx.enter_context(nc.semaphore(n))
        sb = lambda n, s, dt=F32: ctx.enter_context(nc.sbuf_tensor(n, s, dt))
        logits, meta, owner = t["logits"], t["meta"], t["owner"]
        ex, p, mask, one, work = (sb(n, [P, NTILE, NR]) for n in ("ex", "prob", "mask", "one", "work"))
        mx, sm, rs, pm, taken, ss, pos = (sb(n, [P, NTILE]) for n in ("mx", "sm", "rs", "pm", "taken", "ss", "pos"))
        below, ones, each128, kidx = sb("below", [P, P]), sb("ones", [P, P]), sb("each128", [P, NTILE]), sb("kidx", [P, SLOT_TILES])
        incl, more = sb("incl", [P, NR, NTILE]), sb("more", [P, NR, NTILE])
        nt, tend, base, own = sb("nt", [P, NR]), sb("tend", [P, NR]), sb("base", [P, NR]), sb("own", [P, SLOT_TILES])
        posi, lane, slot = sb("posi", [P, NTILE], I32), sb("lane", [P, NTILE], I32), sb("slot", [P, NTILE], I32)
        info, slots = sb("info", [P, NTILE, 2], I32), sb("slots", [P, SLOT_TILES, 2], I32)
        prefix, total = (ctx.enter_context(nc.psum_tensor(n, [P, NTILE, NR], F32)) for n in ("prefix", "total"))
        consts, tri, step, exped, counted = sem("consts"), sem("tri"), sem("step"), sem("exped"), sem("counted")
        onehot, slots_ready, scattered, loaded = sem("onehot"), sem("slots_ready"), sem("scattered"), sem("loaded")
        shifted = sem("shifted")
        block = ctx.enter_context(nc.Block())

        @block.gpsimd
        def _(pool):
            nc.gpsimd.memset(below[:], 1.0).then_inc(tri, 1)
            nc.gpsimd.memset(ones[:], 1.0).then_inc(consts, 1)
            nc.gpsimd.iota(each128[:], pattern=[[P, NTILE]], base=0, channel_multiplier=0, allow_small_or_imprecise_dtypes=True).then_inc(consts, 1)
            nc.gpsimd.iota(kidx[:], pattern=[[1, SLOT_TILES]], base=0, channel_multiplier=0, allow_small_or_imprecise_dtypes=True).then_inc(consts, 1)
            nc.gpsimd.iota(info[:, :, 0], pattern=[[P, NTILE]], base=0, channel_multiplier=1).then_inc(consts, 1)
            pool.wait_ge(tri, 1)
            nc.gpsimd.affine_select(out=below[:], in_=below[:], compare_op=ALU.is_gt, fill=0.0, base=0,
                                    pattern=[[1, P]], channel_multiplier=-1).then_inc(consts, 1)
            pool.wait_ge(slots_ready, 1)
            pool.wait_ge(consts, 5)
            for j in range(NTILE):
                nc.gpsimd.indirect_dma_start(slots_dram, bass.IndirectOffsetOnAxis(slot[:, j:j + 1], 0), info[:, j, :], None).then_inc(scattered, 16)

        @block.sync
        def _(sp):
            sp.wait_ge(scattered, 16 * NTILE)
            sp.dma_start(slots[:], slots_dram.rearrange("(p k) w -> p k w", p=P)).then_inc(loaded, 16)
            sp.wait_ge(loaded, 16)

        @block.scalar
        def _(act):
            act.wait_ge(shifted, 1)
            nc.scalar.activation(ex[:], ex[:], ACT.Exp).then_inc(exped, 1)

        @block.tensor
        def _(pe):
            pe.wait_ge(onehot, 1)
            pe.wait_ge(consts, 5)
            flat = lambda x: x[:].rearrange("p j e -> p (j e)")
            nc.tensor.matmul(flat(prefix), below[:], flat(one), start=True, stop=True)
            nc.tensor.matmul(flat(total), ones[:], flat(one), start=True, stop=True).then_inc(counted, 1)

        @block.vector
        def _(dve):
            done = [0]

            def link(ins):
                done[0] += 1
                ins.then_inc(step, 1)
                dve.wait_ge(step, done[0])

            wide = lambda x: x[:].unsqueeze(2).to_broadcast([P, NTILE, NR])
            v = nc.vector
            routed = logits[:, :, 0:NR]
            link(v.tensor_reduce(mx[:], routed, AX_X, ALU.max))
            v.tensor_tensor(ex[:], routed, wide(mx), ALU.subtract).then_inc(shifted, 1)
            dve.wait_ge(exped, 1)
            link(v.tensor_reduce(sm[:], ex[:], AX_X, ALU.add))
            link(v.reciprocal(rs[:], sm[:]))
            link(v.tensor_tensor(p[:], ex[:], wide(rs), ALU.mult))
            link(v.tensor_reduce(pm[:], p[:], AX_X, ALU.max))
            link(v.tensor_tensor(mask[:], p[:], wide(pm), ALU.is_ge))
            link(v.tensor_copy(taken[:], mask[:, :, 0]))
            link(v.tensor_copy(one[:, :, 0], mask[:, :, 0]))
            for e in range(1, NR - 1):
                link(v.tensor_tensor(one[:, :, e], mask[:, :, e], taken[:], ALU.is_gt))
                link(v.tensor_tensor(taken[:], taken[:], mask[:, :, e], ALU.max))
            link(v.tensor_scalar(one[:, :, NR - 1], taken[:], -1.0, 1.0, ALU.mult, ALU.add))
            v.tensor_copy(work[:], one[:]).then_inc(onehot, 1)
            dve.wait_ge(onehot, 1)
            link(v.tensor_tensor(work[:], p[:], one[:], ALU.mult))
            link(v.tensor_reduce(ss[:], work[:], AX_X, ALU.add))
            link(v.reciprocal(rs[:], ss[:]))
            dve.wait_ge(consts, 5)
            link(v.tensor_tensor(info[:].bitcast(F32)[:, :, 1], ss[:], rs[:], ALU.mult))
            dve.wait_ge(counted, 1)
            for e in range(NR):
                link(v.tensor_tensor_scan(incl[:, e, :], ones[:, 0:NTILE], total[:, :, e], 0.0, ALU.mult, ALU.add))
            for e in range(NR):
                link(v.tensor_scalar(more[:, e, :], each128[:], incl[:, e, NTILE - 1:NTILE], None, ALU.is_lt))
            link(v.tensor_reduce(nt[:], more[:], AX_X, ALU.add))
            link(v.tensor_tensor_scan(tend[:], ones[:, 0:NR], nt[:], 0.0, ALU.mult, ALU.add))
            link(v.tensor_tensor(base[:], tend[:], nt[:], ALU.subtract))
            link(v.tensor_scalar(base[:], base[:], float(P), None, ALU.mult))
            link(v.tensor_tensor(work[:], prefix[:], incl[:].rearrange("p e j -> p j e"), ALU.add))
            link(v.tensor_tensor(work[:], work[:], total[:], ALU.subtract))
            link(v.tensor_tensor(work[:], work[:], base[:].unsqueeze(1).to_broadcast([P, NTILE, NR]), ALU.add))
            link(v.tensor_tensor(work[:], work[:], one[:], ALU.mult))
            link(v.tensor_reduce(pos[:], work[:], AX_X, ALU.add))
            link(v.tensor_copy(posi[:], pos[:]))
            link(v.tensor_scalar(lane[:], posi[:], P - 1, None, ALU.bitwise_and))
            link(v.tensor_scalar(posi[:], posi[:], P.bit_length() - 1, None, ALU.logical_shift_right))
            v.scalar_tensor_tensor(out=slot[:], in0=lane[:], scalar=float(SLOT_TILES), in1=posi[:], op0=ALU.mult, op1=ALU.add).then_inc(slots_ready, 1)
            link(v.tensor_scalar(own[:], kidx[:], tend[:, 0:1], None, ALU.is_ge))
            for e in range(1, NR):
                link(v.scalar_tensor_tensor(out=own[:], in0=kidx[:], scalar=tend[:, e:e + 1], in1=own[:], op0=ALU.is_ge, op1=ALU.add))
            link(v.tensor_scalar(owner[:], own[:], float(NR - 1), None, ALU.min))
            dve.wait_ge(loaded, 16)
            link(v.tensor_scalar(meta[:, :, 0], slots[:, :, 0], float(BATCH * SEQ - 1), None, ALU.min))
            link(v.tensor_scalar(meta[:, :, 1], meta[:, :, 0], SEQ.bit_length() - 1, None, ALU.logical_shift_right))
            link(v.tensor_copy(meta[:, :, 2:4], slots[:]))


def experts_program(nc, t, rows_dram, gb_dram, out):
    NB, AHEAD = 6, 4
    with ExitStack() as ctx:
        sem = lambda n: ctx.enter_context(nc.semaphore(n))
        sb = lambda n, s, dt=F32: ctx.enter_context(nc.sbuf_tensor(n, s, dt))
        ps = lambda n, s: ctx.enter_context(nc.psum_tensor(n, s, F32))
        cur, rows, gbr = sb("cur", [P, NB, 4], I32), sb("rows_sb", [P, NB, 2 * D]), sb("gbr", [P, NB, D])
        outr = sb("outr", [P, NB, D])
        hT, sg, hid, hidT = sb("hT5", [P, 2, KD, P]), sb("sg5", [P, 2, H]), sb("hid5", [P, 2, H]), sb("hidT5", [P, 2, KI, P])
        z = ps("z5", [P, 2, 2, H])
        t_ps, ht_ps, y_ps = ps("t5_ps", [P, KD, P]), ps("ht5_ps", [P, KI, P]), ps("y5_ps", [P, D])
        held = sem("held5")
        cur_ready, fetched = sem("cur_ready"), [sem(f"fetched{i}") for i in range(NB)]
        turned, hT_ready, z_made, silu_ready = sem("turned5"), sem("hT5_ready"), sem("z5_made"), sem("silu5_ready")
        hid_ready, hid_turned, hidT_ready, y_made = sem("hid5_ready"), sem("hid5_turned"), sem("hidT5_ready"), sem("y5_made")
        y_used, out_ready, stored = sem("y5_used"), sem("out5_ready"), [sem(f"stored{i}") for i in range(NB)]
        block = ctx.enter_context(nc.Block())
        N = SLOT_TILES
        first = lambda k, n: isinstance(k, int) and k < n

        def tile_at(k, d):
            if isinstance(k, int):
                return k + d, (k + d) % NB, (k + d) // NB
            return k + d, (2 + d) % NB, (k - 2) // NB + (2 + d) // NB

        def bodies(eng, body, straight=(SLOT_TILES - 2) % NB):
            for k in range(2):
                body(lambda d: tile_at(k, d))
            with eng.Fori(2, N - straight - NB + 1, NB) as k:
                for i in range(NB):
                    body(lambda d: tile_at(k, i + d))
            for k in range(N - straight, N):
                body(lambda d: tile_at(k, d))

        is_last = lambda k, n: isinstance(k, int) and k >= N - n

        @block.gpsimd
        def _(pool):
            def fetch(k, q, n):
                if not first(k, NB):
                    pool.wait_ge(stored[q], 16 * n)
                nc.gpsimd.tensor_copy(cur[:, q, :], t["meta"][:, k, :]).then_inc(cur_ready, 1)
                hold(pool, cur_ready, k + 1, held)
                nc.gpsimd.indirect_dma_start(rows[:, q, :], None, rows_dram, bass.IndirectOffsetOnAxis(cur[:, q, 0:1], 0)).then_inc(fetched[q], 16)
                nc.gpsimd.indirect_dma_start(gbr[:, q, :], None, gb_dram, bass.IndirectOffsetOnAxis(cur[:, q, 1:2], 0)).then_inc(fetched[q], 16)

            def store(k, q, n):
                hold(pool, out_ready, k + 1, held)
                nc.gpsimd.indirect_dma_start(out, bass.IndirectOffsetOnAxis(cur[:, q, 2:3], 0), outr[:, q, :], None,
                                             bounds_check=BATCH * SEQ - 1, oob_is_err=False).then_inc(stored[q], 16)

            def body(at):
                if not first(at(0)[0], 1):
                    store(*at(-1))
                if not is_last(at(0)[0], AHEAD):
                    fetch(*at(AHEAD))

            for k in range(AHEAD):
                fetch(*tile_at(k, 0))
            bodies(pool, body, straight=(N - 2) % NB + NB)
            store(*tile_at(N - 1, 0))
            for q in range(NB):
                pool.wait_ge(stored[q], 16 * ((N - 1 - q) // NB + 1))

        @block.tensor
        def _(pe):
            def turn(k, q, n):
                pe.wait_ge(fetched[q], 32 * n + 32)
                if not first(k, 1):
                    pe.wait_ge(hT_ready, k)
                for i in range(KD):
                    last = nc.tensor.transpose(t_ps[:, i, :], rows[:, q, i * P:(i + 1) * P], t["ident"][:])
                last.then_inc(turned, 1)

            def expert_in(k, q):
                e = pe.value_load(t["owner"][0:1, bass.ds(k, 1)], min_val=0, max_val=NR - 1)
                pe.wait_ge(hT_ready, k + 1)
                if not first(k, 2):
                    pe.wait_ge(hid_ready, k - 1)
                for half in range(2):
                    for i in range(KD):
                        last = nc.tensor.matmul(z[:, q % 2, half, :], hT[:, q % 2, i, :], t["w1r"][:, e, i, half * H:(half + 1) * H],
                                                start=(i == 0), stop=(i == KD - 1))
                last.then_inc(z_made, 1)

            def turn_hid(k, q):
                pe.wait_ge(hid_ready, k + 1)
                if not first(k, 1):
                    pe.wait_ge(hidT_ready, k)
                for i in range(KI):
                    last = nc.tensor.transpose(ht_ps[:, i, :], hid[:, q % 2, i * P:(i + 1) * P], t["ident"][:])
                last.then_inc(hid_turned, 1)

            def expert_out(k, q):
                e = pe.value_load(t["owner"][0:1, bass.ds(k, 1)], min_val=0, max_val=NR - 1)
                pe.wait_ge(hidT_ready, k + 1)
                if not first(k, 1):
                    pe.wait_ge(y_used, k)
                for i in range(KI):
                    last = nc.tensor.matmul(y_ps[:, :], hidT[:, q % 2, i, :], t["w2r"][:, e, i, :], start=(i == 0), stop=(i == KI - 1))
                last.then_inc(y_made, 1)

            def body(at):
                k, q, n = at(0)
                if not first(k, 2):
                    expert_out(*at(-2)[:2])
                if not is_last(k, 1):
                    turn(*at(1))
                if not first(k, 1):
                    turn_hid(*at(-1)[:2])
                expert_in(k, q)

            turn(0, 0, 0)
            bodies(pe, body)
            expert_out(N - 2, (N - 2) % NB)
            turn_hid(N - 1, (N - 1) % NB)
            expert_out(N - 1, (N - 1) % NB)

        @block.scalar
        def _(act):
            def keep_turned(k, q):
                act.wait_ge(turned, k + 1)
                if not first(k, 2):
                    act.wait_ge(z_made, k - 1)
                nc.scalar.activation(hT[:, q % 2], t_ps[:], ACT.Copy).then_inc(hT_ready, 1)

            def keep_hid(k, q):
                act.wait_ge(hid_turned, k + 1)
                if not first(k, 2):
                    act.wait_ge(y_made, k - 1)
                nc.scalar.activation(hidT[:, q % 2], ht_ps[:], ACT.Copy).then_inc(hidT_ready, 1)

            def body(at):
                k, q, n = at(0)
                if not first(k, 1):
                    keep_hid(*at(-1)[:2])
                if not is_last(k, 1):
                    keep_turned(k + 1, (q + 1) % NB)
                act.wait_ge(z_made, k + 1)
                if not first(k, 2):
                    act.wait_ge(hid_ready, k - 1)
                nc.scalar.activation(sg[:, q % 2, :], z[:, q % 2, 1, :], ACT.Silu).then_inc(silu_ready, 1)

            keep_turned(0, 0)
            bodies(act, body)
            keep_hid(N - 1, (N - 1) % NB)

        @block.vector
        def _(dve):
            def combine(k, q, n):
                dve.wait_ge(y_made, k + 1)
                dve.wait_ge(fetched[q], 32 * n + 32)
                nc.vector.scalar_tensor_tensor(out=outr[:, q, :], in0=y_ps[:, :], scalar=cur[:, q, 3:4].bitcast(F32), in1=gbr[:, q, :],
                                               op0=ALU.mult, op1=ALU.mult).then_inc(y_used, 1)
                dve.wait_ge(y_used, k + 1)
                nc.vector.tensor_tensor(outr[:, q, :], outr[:, q, :], rows[:, q, D:2 * D], ALU.add).then_inc(out_ready, 1)

            def body(at):
                k, q, n = at(0)
                dve.wait_ge(silu_ready, k + 1)
                if not first(k, 2):
                    dve.wait_ge(hid_turned, k - 1)
                nc.vector.tensor_tensor(hid[:, q % 2, :], z[:, q % 2, 0, :], sg[:, q % 2, :], ALU.mult).then_inc(hid_ready, 1)
                if not first(k, 1):
                    combine(*at(-1))

            bodies(dve, body)
            combine(*tile_at(N - 1, 0))


def build(nc, ins, out):
    dram = lambda n, s: nc.dram_tensor(n, s, F32, kind="Internal").ap()
    mod2_dram = dram("mod2_rows", [P, 3, BATCH, D])
    gb_dram, rows_dram = dram("gb_rows", [BATCH, D]), dram("token_rows", [BATCH * SEQ, 2 * D])
    slots_dram = nc.dram_tensor("slots_list", [P * SLOT_TILES, 2], I32, kind="Internal").ap()
    bc_dram, x1_dram = dram("bc_rows", [2 * STATE, T]), dram("x1", [BATCH * SEQ, D])
    with ExitStack() as ctx:
        sb = lambda n, s: ctx.enter_context(nc.sbuf_tensor(n, s, F32))
        keep = {"ident": sb("ident", [P, P]), "mhalf": sb("mhalf", [P, 8])}
        with ExitStack() as inner:
            sb = lambda n, s: inner.enter_context(nc.sbuf_tensor(n, s, F32))
            t = keep | {
                "gather": sb("gather", [P, DS]), "limits": sb("limits", [P, NCHUNK + 1, 2]), "state": sb("state", [P, NSET * NG]), "xpad": sb("xpad", [P, KI, T + KCONV - 1]),
                "a": sb("a", [P, NSET * NG]), "cw": sb("cw", [P, KI, KCONV]), "cb": sb("cb", [P, KI]), "dtb": sb("dtb", [P, KI]),
                "w_in": sb("w_in", [P, KD, 2 * DI]), "w_x": sb("w_x", [P, KI, PROJ]), "w_dt": sb("w_dt", [DT_RANK, DI]),
                "w_out": sb("w_out", [P, KI, D]), "w_conv": sb("w_conv", [P, KI, KCONV, P]), "sa": sb("sa", [P, KD, BATCH]),
                "ca": sb("ca", [P, KD, BATCH]), "ga": sb("ga", [P, BATCH, D])}
            setup_program(nc, ins, t, mod2_dram, gb_dram)
            mamba_program(nc, ins, t, bc_dram, x1_dram)
        with ExitStack() as inner:
            sb = lambda n, s, dt=F32: inner.enter_context(nc.sbuf_tensor(n, s, dt))
            t = keep | {"w1r": sb("w1r", [P, NR, KD, 2 * H]), "w2r": sb("w2r", [P, NR, KI, D]), "logits": sb("logits", [P, NTILE, NEXP]),
                        "meta": sb("meta", [P, SLOT_TILES, 4], I32), "owner": sb("owner", [P, SLOT_TILES], I32)}
            shared_program(nc, ins, t, mod2_dram, x1_dram, rows_dram, slots_dram)
            routing_program(nc, t, slots_dram)
            experts_program(nc, t, rows_dram, gb_dram, out)



def laid_out(x):
    import numpy as np
    a = {k: np.asarray(v) for k, v in x.items()}
    c = np.ascontiguousarray
    by_group = lambda w: w.reshape(KI, SPC, DS, -1).transpose(1, 0, 2, 3).reshape(DI, -1)
    return {
        "x": c(a["L0_attn_x"].reshape(BATCH * SEQ, D)),
        "w_in": c(np.concatenate([a["L0_attn_in_proj_w"][:DI], by_group(a["L0_attn_in_proj_w"][DI:])]).T), "conv_w": c(a["L0_attn_conv_w"].reshape(KI, P, KCONV).transpose(1, 0, 2)),
        "conv_b": c(a["L0_attn_conv_b"].reshape(KI, P).T),
        "w_x": c(a["L0_attn_x_proj_w"].T), "w_dt": c(a["L0_attn_dt_proj_w"].T), "dt_b": c(a["L0_attn_dt_proj_b"].reshape(KI, P).T),
        "a_cols": c(a["L0_attn_A_log"].reshape(KI, SPC, DS, NF, NG).transpose(3, 2, 1, 0, 4).reshape(P, NSET * NG)),
        "w_out": c(by_group(a["L0_attn_out_proj_w"].T)), "wg": c(a["L0_ffn_Wg_DN"]), "w1": c(a["L0_ffn_Wl1_ND2H"]), "w2": c(a["L0_ffn_Wl2_NHD"]),
        "c": c(a["L0_c"].reshape(BATCH, KD, P).transpose(2, 1, 0)), "wmod": c(a["L0_wmod"]),
    }


def kernel(**inputs):
    import concourse.bacc as bacc
    from concourse.bass_utils import run_bass_kernel_spmd

    arrays = {f"in_{k}": v for k, v in laid_out(inputs).items()}
    nc = bacc.Bacc("TRN2", target_bir_lowering=False, num_devices=1)
    ins = {k[3:]: nc.dram_tensor(k, v.shape, mybir.dt.from_np(v.dtype), kind="ExternalInput").ap() for k, v in arrays.items()}
    out = nc.dram_tensor("out", [BATCH * SEQ, D], F32, kind="ExternalOutput").ap()
    build(nc, ins, out)
    r = run_bass_kernel_spmd(nc, [arrays], core_ids=[0])
    return r.results[0]["out"].reshape(BATCH, SEQ, D)
```
